# Optimizing a Trainium2 kernel written in Bass

```python
import numpy as np
import jax
import jax.numpy as jnp

def _softmax(x, axis=-1):
    return jax.nn.softmax(x, axis=axis)

def _gelu(x):
    return jax.nn.gelu(x, approximate=True)

def _silu(x):
    return jax.nn.silu(x)

def _sigmoid(x):
    return jax.nn.sigmoid(x)

def _layernorm(x, axis=-1, eps=1e-05):
    m = jnp.mean(x, axis=axis, keepdims=True)
    v = jnp.var(x, axis=axis, keepdims=True)
    return (x - m) / jnp.sqrt(v + eps)

def _scatter_add(tgt, idx, src, axis=0):
    return tgt.at[idx].add(src)

def _segment_sum(src, seg, n):
    return jax.ops.segment_sum(src, seg, n)
kernel_name = 'mk_xattn_ffn_d1_seqx_r2_16bc8c'

def setup_inputs(seed: int=0):
    np.random.seed(seed)
    _w = jnp.asarray

    def _rec_inputs():
        import jax
        import jax.numpy as jnp
        _rk = jax.random.key(seed)
        x = -0.0003929 + 0.9999 * jax.random.normal(jax.random.fold_in(_rk, 1), (4, 1024, 1024), jnp.float32)
        _lenS = 1024 - jax.random.randint(jax.random.fold_in(_rk, 7), (4,), 0, max(1, 1024 // 4) + 1, jnp.int32)
        _lenS2 = 1024 - jax.random.randint(jax.random.fold_in(_rk, 8), (4,), 0, max(1, 1024 // 4) + 1, jnp.int32)
        _ctx_2048P = jax.random.normal(jax.random.fold_in(_rk, 11), (4, 16, 1024), jnp.float32)
        _ctx_2048c = jax.random.dirichlet(jax.random.fold_in(_rk, 511), 0.3 * jnp.ones((16,), jnp.float32), (4, 1024))
        _ctx_2048t = jnp.einsum('bsk,bkd->bsd', _ctx_2048c, _ctx_2048P)
        _ctx_2048t = _ctx_2048t * jax.lax.rsqrt(jnp.mean(jnp.square(_ctx_2048t)) + 1e-12) * 0.953939
        ctx_2048 = 2.81802e-05 + 1.00001 * (_ctx_2048t + 0.3 * jax.random.normal(jax.random.fold_in(_rk, 611), (4, 1024, 1024), jnp.float32))
        return (x, ctx_2048)
    x, ctx_2048 = _rec_inputs()

    def _L0_xattn_setup():
        import jax, jax.numpy as jnp
        import numpy as np
        HIDDEN = 1024
        NUM_HEADS = 16
        HEAD_DIM = HIDDEN // NUM_HEADS
        CHUNK = 512
        SCALE = HEAD_DIM ** (-0.5)

        def _chunked_causal_attention(q, k, v):
            B, H, S, D = q.shape
            n_chunks = S // CHUNK
            kc = k.reshape(B, H, n_chunks, CHUNK, D).transpose(2, 0, 1, 3, 4)
            vc = v.reshape(B, H, n_chunks, CHUNK, D).transpose(2, 0, 1, 3, 4)
            j0s = jnp.arange(n_chunks) * CHUNK
            q_idx = jnp.arange(S)[:, None]
            k_off = jnp.arange(CHUNK)[None, :]
            out0 = jnp.zeros_like(q)
            m0 = jnp.full((B, H, S, 1), -jnp.inf, dtype=q.dtype)
            s0 = jnp.zeros((B, H, S, 1), dtype=q.dtype)

            def step(carry, inputs):
                out, m, s = carry
                kj, vj, j0 = inputs
                scores = jnp.einsum('bhqd,bhkd->bhqk', q, kj) * SCALE
                causal = j0 + k_off > q_idx
                scores = jnp.where(causal[None, None], -jnp.inf, scores)
                chunk_max = scores.max(axis=-1, keepdims=True)
                new_m = jnp.maximum(m, chunk_max)
                exp_old = jnp.exp(m - new_m)
                exp_c = jnp.exp(scores - new_m)
                new_s = s * exp_old + exp_c.sum(axis=-1, keepdims=True)
                out = out * (s / new_s) * exp_old + jnp.einsum('bhqk,bhkd->bhqd', exp_c / new_s, vj)
                return ((out, new_m, new_s), None)
            (out, _, _), _ = jax.lax.scan(step, (out0, m0, s0), (kc, vc, j0s))
            return out
        key = jax.random.key(seed)
        kq, kk, kv = jax.random.split(key, 3)
        B, S = (2, 2048)
        return {'query': jax.random.normal(kq, (B, S, HIDDEN), dtype=jnp.float32), 'key': jax.random.normal(kk, (B, S, HIDDEN), dtype=jnp.float32), 'value': jax.random.normal(kv, (B, S, HIDDEN), dtype=jnp.float32)}
    _L0_xattn_all = _L0_xattn_setup()
    _L0_xattn_in = {k: v for k, v in _L0_xattn_all.items() if k in ()}
    del _L0_xattn_all

    def _L0_ffn_setup():
        import jax, jax.numpy as jnp
        import numpy as np
        NBITS = 4
        OUT_F = 1024
        IN_F = 1024

        def _bit_ste(w, nbits):
            step = float(2 ** nbits - 1)
            w = jnp.clip(w, -1.0, 1.0)
            return jnp.round(jnp.abs(w) * step) / step * jnp.sign(w)
        key = jax.random.key(seed)
        ks = jax.random.split(key, 6)
        ex = np.arange(NBITS - 1, -1, -1)
        exps = jnp.asarray(2.0 ** ex / (2.0 ** NBITS - 1), dtype=jnp.float32)
        inp = {'input': jax.random.normal(ks[0], (8, 1024, IN_F), dtype=jnp.float32), 'pweight': jax.random.normal(ks[1], (OUT_F, IN_F, NBITS), dtype=jnp.float32), 'nweight': jax.random.normal(ks[2], (OUT_F, IN_F, NBITS), dtype=jnp.float32), 'exps': exps, 'bexps': exps, 'mask_weight': jnp.ones((NBITS,), dtype=jnp.float32), 'scale': jnp.array([0.05], dtype=jnp.float32), 'pbias': jax.random.uniform(ks[3], (OUT_F, NBITS), dtype=jnp.float32, minval=0.0, maxval=float(2 ** NBITS - 1)) // 1.0 % 2.0, 'nbias': jax.random.uniform(ks[4], (OUT_F, NBITS), dtype=jnp.float32, minval=0.0, maxval=float(2 ** NBITS - 1)) // 1.0 % 2.0, 'biasscale': jnp.array([0.05], dtype=jnp.float32)}
        return inp
    _L0_ffn_all = _L0_ffn_setup()
    _L0_ffn_in = {k: v for k, v in _L0_ffn_all.items() if k in ('pweight', 'nweight', 'exps', 'bexps', 'mask_weight', 'scale', 'pbias', 'nbias', 'biasscale')}
    del _L0_ffn_all
    return {'x': x, 'ctx_2048': ctx_2048, 'L0_ffn_pweight': _L0_ffn_in['pweight'], 'L0_ffn_nweight': _L0_ffn_in['nweight'], 'L0_ffn_exps': _L0_ffn_in['exps'], 'L0_ffn_bexps': _L0_ffn_in['bexps'], 'L0_ffn_mask_weight': _L0_ffn_in['mask_weight'], 'L0_ffn_scale': _L0_ffn_in['scale'], 'L0_ffn_pbias': _L0_ffn_in['pbias'], 'L0_ffn_nbias': _L0_ffn_in['nbias'], 'L0_ffn_biasscale': _L0_ffn_in['biasscale']}

def reference(x, ctx_2048, L0_ffn_pweight, L0_ffn_nweight, L0_ffn_exps, L0_ffn_bexps, L0_ffn_mask_weight, L0_ffn_scale, L0_ffn_pbias, L0_ffn_nbias, L0_ffn_biasscale):
    import jax
    import jax.numpy as jnp

    def _L0_xattn_ref(query, key, value):
        import jax, jax.numpy as jnp
        import numpy as np
        HIDDEN = 1024
        NUM_HEADS = 16
        HEAD_DIM = HIDDEN // NUM_HEADS
        CHUNK = 512
        SCALE = HEAD_DIM ** (-0.5)

        def _chunked_causal_attention(q, k, v):
            B, H, S, D = q.shape
            n_chunks = S // CHUNK
            kc = k.reshape(B, H, n_chunks, CHUNK, D).transpose(2, 0, 1, 3, 4)
            vc = v.reshape(B, H, n_chunks, CHUNK, D).transpose(2, 0, 1, 3, 4)
            j0s = jnp.arange(n_chunks) * CHUNK
            q_idx = jnp.arange(S)[:, None]
            k_off = jnp.arange(CHUNK)[None, :]
            out0 = jnp.zeros_like(q)
            m0 = jnp.full((B, H, S, 1), -jnp.inf, dtype=q.dtype)
            s0 = jnp.zeros((B, H, S, 1), dtype=q.dtype)

            def step(carry, inputs):
                out, m, s = carry
                kj, vj, j0 = inputs
                scores = jnp.einsum('bhqd,bhkd->bhqk', q, kj) * SCALE
                causal = j0 + k_off > q_idx
                scores = jnp.where(causal[None, None], -jnp.inf, scores)
                chunk_max = scores.max(axis=-1, keepdims=True)
                new_m = jnp.maximum(m, chunk_max)
                exp_old = jnp.exp(m - new_m)
                exp_c = jnp.exp(scores - new_m)
                new_s = s * exp_old + exp_c.sum(axis=-1, keepdims=True)
                out = out * (s / new_s) * exp_old + jnp.einsum('bhqk,bhkd->bhqd', exp_c / new_s, vj)
                return ((out, new_m, new_s), None)
            (out, _, _), _ = jax.lax.scan(step, (out0, m0, s0), (kc, vc, j0s))
            return out
        B, S, _ = query.shape
        q = query.reshape(B, S, NUM_HEADS, HEAD_DIM).transpose(0, 2, 1, 3)
        k = key.reshape(B, S, NUM_HEADS, HEAD_DIM).transpose(0, 2, 1, 3)
        v = value.reshape(B, S, NUM_HEADS, HEAD_DIM).transpose(0, 2, 1, 3)
        out = _chunked_causal_attention(q, k, v)
        return out.transpose(0, 2, 1, 3).reshape(B, S, HIDDEN)

    def _L0_ffn_ref(input, pweight, nweight, exps, bexps, mask_weight, scale, pbias, nbias, biasscale):
        import jax, jax.numpy as jnp
        import numpy as np
        NBITS = 4
        OUT_F = 1024
        IN_F = 1024

        def _bit_ste(w, nbits):
            step = float(2 ** nbits - 1)
            w = jnp.clip(w, -1.0, 1.0)
            return jnp.round(jnp.abs(w) * step) / step * jnp.sign(w)
        temp = 1.0
        mask = jax.nn.sigmoid(mask_weight)
        soft = jax.nn.sigmoid(temp * pweight) - jax.nn.sigmoid(temp * nweight)
        weight = jnp.einsum('oin,n->oi', soft, exps * mask) * scale[0]
        bias_raw = jnp.einsum('on,n->o', pbias - nbias, bexps)
        bias = _bit_ste(bias_raw, NBITS) * biasscale[0]
        return jnp.einsum('bsi,oi->bso', input, weight) + bias
    x = x + _L0_xattn_ref(_layernorm(x, axis=-1), ctx_2048, ctx_2048)
    x = x + _L0_ffn_ref(_layernorm(x, axis=-1), L0_ffn_pweight, L0_ffn_nweight, L0_ffn_exps, L0_ffn_bexps, L0_ffn_mask_weight, L0_ffn_scale, L0_ffn_pbias, L0_ffn_nbias, L0_ffn_biasscale)
    return x

_drawn_inputs = setup_inputs


def setup_inputs(seed=0):
    import zlib

    import numpy as np

    out = dict(_drawn_inputs(seed))
    spreads = {'L0_ffn_mask_weight': (1.0, 0.6)}
    factors = {'L0_ffn_bexps': 4.447, 'L0_ffn_pbias': 4.604, 'L0_ffn_nbias': 4.522}
    for name, (base, spread) in spreads.items():
        noise = np.random.default_rng([zlib.crc32(name.encode()), seed]).standard_normal(out[name].shape)
        drawn = base * np.exp(spread * noise) if base else spread * noise
        out[name] = jnp.asarray(drawn.astype(out[name].dtype))
    for name, factor in factors.items():
        out[name] = (out[name] * factor).astype(out[name].dtype)
    return out
```

```python
import math
from contextlib import ExitStack

import concourse.bass as bass
from concourse import mybir

ALU = mybir.AluOpType
ACT = mybir.ActivationFunctionType
AX_X = mybir.AxisListType.X
F32 = mybir.dt.float32
F16 = mybir.dt.float16
BF16 = mybir.dt.bfloat16

P = 128
B, SEQ, DM = 4, 1024, 1024
NT = SEQ // P
H, D = 16, 64
KT_N = DM // P
NBITS = 4
EPS = 1e-5
SCALE = D ** -0.5
LAG = 5
GROUP = 4
P_SHIFT = 10 * math.log(2)
MASKED = -1e30
ROUND = 1.5 * 2 ** 23

HPJ = [4, 4, 2, 2, 1, 1, 1, 1]
JPG = [GROUP // h for h in HPJ]
JOBS = [H // h for h in HPJ]
JOB0 = [sum(JOBS[:i]) for i in range(NT + 1)]
HEAD_STRIDE = [128, 256, 512, 512, 1024, 1024, 1024, 1024]


def uses_of(first):
    seq = [("S", 0, 0)]
    for i in range(NT):
        last_looped = 3 * JPG[i] + 1
        mid = [("QT", i), ("KT", i)] + ([] if first and i < LAG else [("YT", i)])
        ffn = [] if first and i < LAG else [("FFN", i)]
        w = [("WT", 2 * i), ("WT", 2 * i + 1)] if first and i < 4 else []
        seq += [("S", i, q) for q in range(1, min(last_looped, JOBS[i] - 1) + 1)]
        if i < NT - 1:
            seq += mid + [("S", i, q) for q in range(last_looped + 1, JOBS[i])] + [("S", i + 1, 0)] + w + ffn
        else:
            seq += [("S", i, q) for q in range(last_looped + 1, JOBS[i])] + mid + ffn
    return {u: n for n, u in enumerate(seq)}


USE_FIRST, USE_LATER = uses_of(True), uses_of(False)
USE_BASE = 3
USE_LATER_BASE = USE_BASE + len(USE_FIRST)


class Use:

    def __init__(self, const, run=0):
        self.const, self.run = const, run
        self.slot = const % 2
        self.filled = const + run + 1
        self.released = const - const % 2 + 2 + run
        self.free = const - const % 2 + run
        self.wait_free = not (isinstance(run, int) and const + run < 2)


def use(b, *key):
    if isinstance(b, int) and b == 0:
        return Use(USE_BASE + USE_FIRST[key])
    return Use(USE_LATER_BASE - len(USE_LATER) + USE_LATER[key], len(USE_LATER) * b)


class Job:

    def __init__(self, b, i, s, g=0):
        self.b, self.i, self.s, self.g = b, i, s, g
        static = isinstance(g, int)
        q = JPG[i] * g + s
        self.heads = HPJ[i]
        self.blocks = self.heads * (i + 1)
        self.chunks = (self.blocks + 3) // 4
        self.keys = (i + 1) * P
        self.head0 = GROUP * g + HPJ[i] * s
        self.number = b * JOB0[NT] + JOB0[i] + q
        self.par = (q if static else s) % 2
        self.number1 = b * (JOB0[NT] - JOBS[0]) + JOB0[i] - JOBS[0] + q
        self.first_of_tile = static and q == 0
        if static:
            self.use = use(b, "S", i, q)
        else:
            u = use(b, "S", i, s if s else 1)
            self.use = Use(u.const - (0 if s else 1), u.run + JPG[i] * g)

    def chunk_number(self, c):
        return self.number1 if c else self.number

    def next(self):
        if isinstance(self.g, int) and JPG[self.i] * self.g + self.s + 1 == JOBS[self.i]:
            return first_job(self.b, self.i + 1)
        return Job(self.b, self.i, self.s + 1, self.g)


def first_job(b, i):
    if i < NT:
        return Job(b, i, 0)
    j = Job(b, 0, 0)
    j.number = b * JOB0[NT] + JOB0[NT]
    j.use = Use(USE_LATER_BASE) if isinstance(b, int) and b == 0 else Use(
        USE_LATER_BASE, len(USE_LATER) * b)
    return j


def group_loop(eng, i, body):
    if JPG[i] == 1:
        for g in range(3):
            body(g)
    else:
        with eng.Fori(0, 3) as g:
            body(g)


def batches(eng, section):
    for i in range(NT):
        section(0, i)
    with eng.Fori(1, B) as b:
        for i in range(NT):
            section(b, i)


def build(nc, x, ctx_in, pweight, nweight, exps, bexps, mask_weight, scale, pbias, nbias, biasscale, out):
    x_t = x.rearrange("b (i p) d -> (b i) p d", p=P)
    c_t = ctx_in.rearrange("b (i p) d -> (b i) p d", p=P)
    out_t = out.rearrange("b (i p) d -> (b i) p d", p=P)
    WCH = 128
    NWCH = DM // WCH
    pw_t = pweight.rearrange("(o p) (c k) n -> o c p (k n)", p=P, k=WCH)
    nw_t = nweight.rearrange("(o p) (c k) n -> o c p (k n)", p=P, k=WCH)

    with ExitStack() as stack:
        def sb(name, shape, dt):
            return stack.enter_context(nc.sbuf_tensor(name, shape, dt))

        def sem(name):
            return stack.enter_context(nc.semaphore(name))

        wt = sb("wt", [P, 2, KT_N, DM], F16)
        v16 = sb("v16", [P, NT, H, 2 * D], F16)
        kt16 = sb("kt16", [P, NT, H, P], F16)
        ring = sb("ring", [P, NT, DM], F32)
        cin = sb("cin", [P, 2, DM], F32)
        c16 = sb("c16", [P, 2, H, 2 * D], F16)
        norm32 = sb("norm32", [P, DM], F32)
        q16 = sb("q16", [P, H, 2 * D], F16)
        qt = sb("qt", [P, 2, H, P], F16)
        qs = sb("qs", [P, 2, H, P], F16)
        p32 = sb("p32", [P, 2, 8 * P], F32)
        pt_hi = sb("pt_hi", [P, 2, 8 * P], F16)
        pt_lo = sb("pt_lo", [P, 2, 8 * P], F16)
        olo = sb("olo", [P, GROUP, D], F32)
        att = sb("att", [P, GROUP, D], F32)
        y16 = sb("y16", [P, 2, KT_N, P], F16)
        yt = sb("yt", [P, 2, KT_N, P], F16)
        xb = sb("xb", [P, 2, DM], F32)
        bias_row = sb("bias_row", [P, DM], F32)
        wp = xb[:, 0, :].rearrange("p (r f) -> p r f", r=2)
        wn = xb[:, 1, :].rearrange("p (r f) -> p r f", r=2)
        w32 = yt[:, :, :, :].bitcast(F32).rearrange("p a b c -> p (a b c)")
        ones32 = y16[:, 0, 0:2, :].bitcast(F32).rearrange("p a b -> p (a b)")
        id32 = sb("id32", [P, P], F32)
        id16 = sb("id16", [P, P], F16)
        idb = sb("idb", [P, P], BF16)
        maskb = sb("maskb", [P, P], BF16)
        half_neg = sb("half_neg", [P, 1], F32)
        gate = sb("gate", [P, 8], F32)
        mx = sb("mx", [P, 2, GROUP], F32)
        nb = sb("nb", [P, 2, GROUP], F32)
        rowsum = sb("rowsum", [P, 2, H], F32)
        rinv = sb("rinv", [P, GROUP], F32)
        stats = sb("stats", [P, 2, 12], F32)
        mv = sb("mv", [P, 2, 2], F32)
        rstd = sb("rstd", [P, 2, 3], F32)
        small = sb("small", [P, 18], F32)
        coef = small[:, 14:18]
        bits = y16[:, 1, 0, :].bitcast(F32).rearrange("p (a n) -> p a n", a=2)
        bvec = sb("bvec", [P, 8], F32)
        bdiag = norm32[:, :].rearrange("p (j q) -> p j q", j=8)

        slot = stack.enter_context(nc.psum_tensor("slot", [P, 2, 1024], F32))
        ptb = stack.enter_context(nc.psum_tensor("ptb", [P, 2, 512], F32))
        oacc = stack.enter_context(nc.psum_tensor("oacc", [P, 8 * 2 * D], F32))
        slot16 = slot[:, :, :].bitcast(F16).rearrange("p s (k c) -> p s k c", c=P)

        x_in = [sem(f"x_in{r}") for r in range(4)]
        c_in = [sem(f"c_in{r}") for r in range(2)]
        v_in = [sem(f"v_in{r}") for r in range(2)]
        qs_in = [sem(f"qs_in{r}") for r in range(2)]
        w_in = [sem(f"w_in{r}") for r in range(2)]
        out_done = [sem(f"out_done{r}") for r in range(2)]
        small_in = sem("small_in")
        slot_filled = sem("slot_filled")
        slot_released = [sem(f"slot_released{r}") for r in range(2)]
        mx_ready = sem("mx_ready")
        nb_ready = sem("nb_ready")
        pt_filled = [sem(f"pt_filled{c}") for c in range(2)]
        hi_ready = [sem(f"hi_ready{c}") for c in range(2)]
        lo_ready = [sem(f"lo_ready{c}") for c in range(2)]
        pv_done = sem("pv_done")
        rinv_ready = sem("rinv_ready")
        olo_ready = sem("olo_ready")
        osum_ready = sem("osum_ready")
        att_ready = sem("att_ready")
        x1_ready = sem("x1_ready")
        q_stats, q_mv, q_rs, q_norm, q_hi, q_lo = (sem("q_" + n) for n in ("stats", "mv", "rs", "norm", "hi", "lo"))
        c_hi, c_lo = sem("c_hi"), sem("c_lo")
        y_stats, y_mv, y_rs, y_norm, y_hi, y_lo = (sem("y_" + n) for n in ("stats", "mv", "rs", "norm", "hi", "lo"))
        xb_ready = sem("xb_ready")
        pool_const = sem("pool_const")
        th_ready, d_ready, w_step, w_hi, w_lo = (sem("w_" + n) for n in ("tanh", "diff", "step", "hi", "lo"))
        coef_tanh = sem("coef_tanh")
        coef_step = sem("coef_step")
        bias_step = sem("bias_step")

        def tile(b, i):
            return NT * b + i

        def dve_wait_apart(column, s, value):
            nc.vector.wait_ge(s, value)
            nc.vector.memset(gate[:, column:column + 1], 0.0)

        def pool_wait_apart(column, s, value):
            nc.gpsimd.wait_ge(s, value)
            nc.gpsimd.tensor_tensor(gate[:, column:column + 1], half_neg[:, :], half_neg[:, :], ALU.add)

        block = stack.enter_context(nc.Block())

        @block.sync
        def _(sp):
            def load_x(b, k, t):
                if not (isinstance(t, int) and t < NT):
                    sp.wait_ge(xb_ready, t - NT + 1)
                src = x_t[t] if isinstance(t, int) else x_t[bass.ds(t % (B * NT), 1)].rearrange("a p d -> (a p) d")
                sp.dma_start(ring[:, k % NT, :], src).then_inc(x_in[k % 4], 16)

            def load_c(b, k, t):
                if not (isinstance(t, int) and t < 2):
                    sp.wait_ge(c_lo, t - 1)
                src = c_t[t] if isinstance(t, int) else c_t[bass.ds(t % (B * NT), 1)].rearrange("a p d -> (a p) d")
                sp.dma_start(cin[:, k % 2, :], src).then_inc(c_in[k % 2], 16)

            def keep_v(t, i, pv):
                sp.wait_ge(c_lo, t + 1)
                if pv is not None:
                    sp.wait_ge(pv_done, pv)
                sp.dma_start(v16[:, i % NT], c16[:, i % 2]).then_inc(v_in[i % 2], 16)

            def swap(u, i):
                sp.wait_ge(slot_released[u.slot], u.released)
                sp.dma_start(qs[0:D, i % 2], qt[D:P, i % 2]).then_inc(qs_in[i % 2], 16)
                sp.dma_start(qs[D:P, i % 2], qt[0:D, i % 2]).then_inc(qs_in[i % 2], 16)

            def load_w(n):
                if n >= 2:
                    sp.wait_ge(w_step, NBITS * (n - 1))
                sp.dma_start(wp[:, n % 2], pw_t[n // NWCH, n % NWCH]).then_inc(w_in[n % 2], 16)
                sp.dma_start(wn[:, n % 2], nw_t[n // NWCH, n % NWCH]).then_inc(w_in[n % 2], 16)

            for at, src in ((0, exps), (4, bexps), (8, mask_weight), (12, scale), (13, biasscale)):
                n = src.shape[0]
                sp.dma_start(small[:, at:at + n], src.rearrange("(a n) -> a n", a=1).to_broadcast([P, n])
                             ).then_inc(small_in, 16)
            for k, src in enumerate((pbias, nbias)):
                sp.dma_start(bits[:, k, :], src.rearrange("(p j) n -> p (j n)", p=P)).then_inc(small_in, 16)
            for t in range(2):
                load_x(0, t, t)
                load_c(0, t, t)
            load_x(0, 2, 2)
            load_c(0, 2, 2)
            swap(Use(1), 0)
            keep_v(0, 0, None)

            def section(b, i):
                t = tile(b, i)
                load_x(b, i + 3, t + 3)
                load_c(b, i + 3, t + 3)
                if i < NT - 1:
                    keep_v(t + 1, i + 1, None)
                swap(use(b, "QT", i), i + 1)
                if i == NT - 1:
                    keep_v(t + 1, i + 1, b * JOB0[NT] + JOB0[NT])
                if isinstance(b, int) and b == 0:
                    if i < 4:
                        for n in range(2 * i * NWCH, (2 * i + 2) * NWCH):
                            load_w(n)
                    if i >= LAG:
                        store(use(b, "FFN", i), t - LAG, i - LAG)
                else:
                    store(use(b, "FFN", i), t - LAG, i - LAG)

            def store(u, t, k):
                sp.wait_ge(slot_released[u.slot], u.released)
                dst = out_t[t] if isinstance(t, int) else out_t[bass.ds(t, 1)].rearrange("a p d -> (a p) d")
                sp.dma_start(dst, xb[:, k % 2, :]).then_inc(out_done[k % 2], 16)

            batches(sp, section)
            for k in range(LAG):
                t = B * NT - LAG + k
                store(Use(END_USE + 2 * k + 1), t, t)
            for r in range(2):
                sp.wait_ge(out_done[r], 16 * B * NT // 2)

        @block.tensor
        def _(pe):
            def take(u):
                if u.wait_free:
                    pe.wait_ge(slot_released[u.slot], u.free)

            def scores(j):
                i = j.i
                take(j.use)
                for hh in range(j.heads):
                    h = j.head0 + hh
                    base = hh * HEAD_STRIDE[i]
                    for w in range((i + 4) // 4):
                        blocks = min(4, i + 1 - 4 * w)
                        dst = slot[:, j.use.slot, base + 512 * w:base + 512 * w + blocks * P]
                        keys = kt16[:, 4 * w:4 * w + blocks, h, :]
                        diagonal = 4 * w + blocks == i + 1
                        pe.matmul(dst, qt[:, i % 2, h, :], keys, start=True, stop=False, skip_group_check=True)
                        last = pe.matmul(dst, qs[:, i % 2, h, :], keys, start=False, stop=not diagonal,
                                         skip_group_check=True)
                        if diagonal:
                            dst = slot[:, j.use.slot, base + i * P:base + (i + 1) * P]
                            last = pe.matmul(dst, idb[:, :], maskb[:, :], start=False, stop=True,
                                             skip_group_check=True)
                last.then_inc(slot_filled, 1)

            def scores_of_new_tile(b, i, j):
                for name in ("QT", "KT"):
                    u = use(b, name, i)
                    if u.slot != j.use.slot:
                        pe.wait_ge(slot_released[u.slot], u.released)
                n = (i + 1) // 2 + 1 + 4 * b
                pe.wait_ge(qs_in[(i + 1) % 2], 32 * n)
                scores(j)

            def transpose_p(j):
                pe.wait_ge(slot_released[j.use.slot], j.use.released)
                for c in range(j.chunks):
                    n = j.chunk_number(c)
                    if not (isinstance(n, int) and n == 0):
                        pe.wait_ge(lo_ready[c], n)
                    for k in range(4 * c, min(4 * c + 4, j.blocks)):
                        last = pe.transpose(ptb[:, c, (k - 4 * c) * P:(k - 4 * c + 1) * P],
                                            p32[:, j.par, k * P:(k + 1) * P], id32[:, :])
                    last.then_inc(pt_filled[c], 1)

            def values(j, g):
                i = j.i
                if isinstance(j.g, int) and JPG[i] * j.g + j.s == 0:
                    pe.wait_ge(v_in[i % 2], 16 * (i // 2 + 1 + 4 * j.b))
                first_of_group = (j.s % JPG[i] == 0) if isinstance(j.g, int) else j.s == 0
                gn = 4 * tile(j.b, i) + g
                if first_of_group and not (isinstance(gn, int) and gn < 2):
                    pe.wait_ge(osum_ready, gn - 1)
                for c in range(j.chunks):
                    pe.wait_ge(lo_ready[c], j.chunk_number(c) + 1)
                for hh in range(j.heads):
                    h = j.head0 + hh
                    k0 = (HPJ[i] * j.s + hh) % GROUP
                    at = (g % 2) * (GROUP * 2 * D) + k0 * 2 * D
                    for blk in range(i + 1):
                        k = hh * (i + 1) + blk
                        cols = slice(k * P, (k + 1) * P)
                        pe.matmul(oacc[:, bass.ds(at, 2 * D)], pt_hi[:, j.par, cols], v16[:, blk, h, :],
                                  start=blk == 0, stop=False, skip_group_check=True)
                        last = pe.matmul(oacc[:, bass.ds(at, D)], pt_lo[:, j.par, cols], v16[:, blk, h, 0:D],
                                         start=False, stop=blk == i, skip_group_check=True)
                last.then_inc(pv_done, 1)

            def turn(u, src):
                take(u)
                for k in range(16):
                    last = pe.transpose(slot16[:, u.slot, k, :], src(k), id16[:, :])
                last.then_inc(slot_filled, 1)

            def turn_q(u, t):
                pe.wait_ge(q_lo, t + 1)
                turn(u, lambda k: q16[:, k, :])

            def turn_k(u, t, i):
                pe.wait_ge(c_lo, t + 1)
                turn(u, lambda k: c16[:, i % 2, k, :])

            def turn_y(u, t):
                pe.wait_ge(y_lo, t + 1)
                turn(u, lambda k: y16[:, k // KT_N, k % KT_N, :])

            def linear(u, turned):
                take(u)
                if turned.slot != u.slot:
                    pe.wait_ge(slot_released[turned.slot], turned.released)
                terms = ((0, 0), (1, 0), (0, 1))
                for half in range(2):
                    for n, (a, c) in enumerate(terms):
                        for k in range(KT_N):
                            last = pe.matmul(slot[:, u.slot, half * 512:half * 512 + 512], yt[:, a, k, :],
                                             wt[:, c, k, half * 512:half * 512 + 512],
                                             start=n == 0 and k == 0, stop=n == len(terms) - 1 and k == KT_N - 1)
                last.then_inc(slot_filled, 1)

            pe.wait_ge(pool_const, 10)
            pe.wait_ge(bias_step, 18)
            for j in range(8):
                last = pe.matmul(slot[:, 0, j * P:(j + 1) * P], ones32[:, :], bdiag[:, j, :], start=True, stop=True)
            last.then_inc(slot_filled, 1)
            turn_q(Use(1), 0)
            turn_k(Use(2), 0, 0)
            for u in (Use(1), Use(2)):
                pe.wait_ge(slot_released[u.slot], u.released)
            pe.wait_ge(qs_in[0], 32)
            scores(Job(0, 0, 0))

            def section(b, i):
                first = isinstance(b, int) and b == 0
                t = tile(b, i)
                last_job = Job(b, i, JOBS[i] - 1)

                def mid():
                    turn_q(use(b, "QT", i), t + 1)
                    turn_k(use(b, "KT", i), t + 1, i + 1)
                    if not (first and i < LAG):
                        turn_y(use(b, "YT", i), t - LAG)

                def ffn():
                    if not (first and i < LAG):
                        linear(use(b, "FFN", i), use(b, "YT", i))

                scores(Job(b, i, 1))
                transpose_p(Job(b, i, 0))

                def body(g):
                    for s in range(1, JPG[i] + 1):
                        j = Job(b, i, s, g)
                        if not isinstance(g, int) or JPG[i] * g + s + 1 < JOBS[i]:
                            scores(j.next())
                        transpose_p(j)
                        values(Job(b, i, s - 1, g), g)
                group_loop(pe, i, body)
                if i < NT - 1:
                    mid()
                for q in range(3 * JPG[i] + 1, JOBS[i]):
                    j = Job(b, i, q)
                    if q + 1 < JOBS[i]:
                        scores(j.next())
                    transpose_p(j)
                    values(Job(b, i, q - 1), 3)
                if i < NT - 1:
                    scores_of_new_tile(b, i, first_job(b, i + 1))
                    if first and i < 4:
                        for o in (2 * i, 2 * i + 1):
                            pe.wait_ge(w_lo, o + 1)
                            turn(use(b, "WT", o), lambda k: y16[:, k // KT_N, k % KT_N, :])
                    ffn()
                    values(last_job, 3)
                else:
                    mid()
                    values(last_job, 3)
                    ffn()
                    scores_of_new_tile(b, i, first_job(b, i + 1))

            batches(pe, section)
            for k in range(LAG):
                turned = Use(END_USE + 2 * k)
                turn_y(turned, B * NT - LAG + k)
                linear(Use(END_USE + 2 * k + 1), turned)

        @block.scalar
        def _(act):
            def exponentials(j):
                act.wait_ge(nb_ready, j.number + 1)
                for hh in range(j.heads):
                    base = hh * HEAD_STRIDE[j.i]
                    last = nc.scalar.activation(
                        p32[:, j.par, hh * j.keys:(hh + 1) * j.keys], slot[:, j.use.slot, base:base + j.keys],
                        ACT.Exp, bias=nb[:, j.par, hh:hh + 1], scale=SCALE,
                        accum_out=rowsum[:, j.i % 2, bass.ds(j.head0 + hh, 1)])
                last.then_inc(slot_released[j.use.slot], 2)

            def high_parts(j):
                if not (isinstance(j.number, int) and j.number < 2):
                    act.wait_ge(pv_done, j.number - 1)
                for c in range(j.chunks):
                    act.wait_ge(pt_filled[c], j.chunk_number(c) + 1)
                    n = (min(4 * c + 4, j.blocks) - 4 * c) * P
                    nc.scalar.copy(pt_hi[:, j.par, 512 * c:512 * c + n], ptb[:, c, 0:n]).then_inc(hi_ready[c], 1)

            def output_low(b, i, g, pv):
                gn = 4 * tile(b, i) + g
                if not (isinstance(gn, int) and gn == 0):
                    act.wait_ge(att_ready, gn)
                act.wait_ge(pv_done, pv)
                src = oacc[:, bass.ds((g % 2) * GROUP * 2 * D, GROUP * 2 * D)].rearrange("p (k c) -> p k c", c=2 * D)
                nc.scalar.copy(olo[:, :, :], src[:, :, D:2 * D]).then_inc(olo_ready, 1)

            def take_first_half(u, dst):
                act.wait_ge(slot_filled, u.filled)
                nc.scalar.copy(dst, slot16[:, u.slot, 0:8, :]).then_inc(slot_released[u.slot], 1)

            def q_split(t, i, turned):
                act.wait_ge(q_norm, t + 1)
                if turned is not None:
                    act.wait_ge(slot_filled, turned.filled)
                nc.scalar.copy(q16[:, :, 0:D], norm32[:, :].rearrange("p (h d) -> p h d", d=D)).then_inc(q_hi, 1)

            def c_split(t, i, turned, n_in):
                act.wait_ge(c_in[i % 2], 16 * n_in)
                if turned is not None:
                    act.wait_ge(slot_filled, turned.filled)
                    act.wait_ge(v_in[i % 2], 16 * (n_in - 1))
                nc.scalar.copy(c16[:, i % 2, :, 0:D], cin[:, i % 2, :].rearrange("p (h d) -> p h d", d=D)
                               ).then_inc(c_hi, 1)

            def y_split(t, turned):
                act.wait_ge(y_norm, t + 1)
                if turned is not None:
                    act.wait_ge(slot_filled, turned.filled)
                nc.scalar.copy(y16[:, 0, :, :], norm32[:, :].rearrange("p (k c) -> p k c", c=P)).then_inc(y_hi, 1)

            act.wait_ge(small_in, 16 * 7)
            nc.scalar.activation(coef, small[:, 8:12], ACT.Tanh, scale=0.5).then_inc(coef_tanh, 1)
            c_split(0, 0, None, 1)
            q_split(0, 0, None)
            act.wait_ge(slot_filled, 1)
            nc.scalar.copy(bias_row[:, :].rearrange("p (q j) -> p j q", j=8)[:, 0:4, :],
                           slot[:, 0, 0:512].rearrange("p (j q) -> p j q", j=4)).then_inc(slot_released[0], 1)
            take_first_half(Use(1), qt[:, 0, 0:8, :])
            take_first_half(Use(2), kt16[:, 0, 0:8, :])
            c_split(1, 1, None, 1)
            q_split(1, 1, Use(1))
            exponentials(Job(0, 0, 0))

            def section(b, i):
                first = isinstance(b, int) and b == 0
                t = tile(b, i)
                last_job = Job(b, i, JOBS[i] - 1)
                jobs0 = b * JOB0[NT] + JOB0[i]

                def mid():
                    take_first_half(use(b, "QT", i), qt[:, (i + 1) % 2, 0:8, :])
                    take_first_half(use(b, "KT", i), kt16[:, (i + 1) % NT, 0:8, :])
                    if not (first and i < LAG):
                        take_first_half(use(b, "YT", i), yt[:, 0, :, :])

                def prepare():
                    if i > 0:
                        c_turned = use(b, "KT", i - 1)
                    elif first:
                        c_turned = Use(2)
                    else:
                        c_turned = Use(USE_LATER_BASE - len(USE_LATER), len(USE_LATER) * b)
                    c_split(t + 2, i + 2, c_turned, (i + 2) // 2 + 1 + 4 * b)
                    q_split(t + 2, i + 2, use(b, "QT", i))
                    if not (first and i < LAG - 1):
                        y_split(t - LAG + 1, None if first and i < LAG else use(b, "YT", i))

                def weights(o):
                    for n in range(o * NWCH, (o + 1) * NWCH):
                        act.wait_ge(w_in[n % 2], 32 * (n // 2 + 1))
                        nc.scalar.activation(wp[:, n % 2], wp[:, n % 2], ACT.Tanh, scale=0.5)
                        nc.scalar.activation(wn[:, n % 2], wn[:, n % 2], ACT.Tanh, scale=0.5).then_inc(th_ready, 1)
                    act.wait_ge(w_step, NBITS * NWCH * (o + 1))
                    if o > 0:
                        act.wait_ge(slot_filled, use(0, "WT", o - 1).filled)
                    nc.scalar.copy(y16[:, 0, :, :], w32.rearrange("p (k c) -> p k c", c=P)).then_inc(w_hi, 1)

                high_parts(Job(b, i, 0))
                exponentials(Job(b, i, 1))

                def body(g):
                    for s in range(1, JPG[i] + 1):
                        j = Job(b, i, s, g)
                        high_parts(j)
                        if not isinstance(g, int) or JPG[i] * g + s + 1 < JOBS[i]:
                            exponentials(j.next())
                    output_low(b, i, g, jobs0 + JPG[i] * (g + 1))
                group_loop(act, i, body)
                if i < NT - 1:
                    mid()
                for q in range(3 * JPG[i] + 1, JOBS[i]):
                    j = Job(b, i, q)
                    high_parts(j)
                    if q + 1 < JOBS[i]:
                        exponentials(j.next())
                if i < NT - 1:
                    exponentials(first_job(b, i + 1))
                    prepare()
                    if first and i < 4:
                        for o in (2 * i, 2 * i + 1):
                            weights(o)
                            take_first_half(use(b, "WT", o), wt[:, 0, :, o * P:(o + 1) * P])
                    output_low(b, i, 3, jobs0 + JOBS[i])
                else:
                    mid()
                    output_low(b, i, 3, jobs0 + JOBS[i])
                    prepare()
                    exponentials(first_job(b, i + 1))

            batches(act, section)
            for k in range(LAG):
                turned = Use(END_USE + 2 * k)
                take_first_half(turned, yt[:, 0, :, :])
                if k < LAG - 1:
                    y_split(B * NT - LAG + k + 1, turned)

        @block.vector
        def _(dve):
            def maxima(j):
                dve.wait_ge(slot_filled, j.use.filled)
                if not (isinstance(j.number, int) and j.number < 2):
                    dve.wait_ge(mx_ready, j.number)
                src = slot[:, j.use.slot, :].rearrange("p (h c) -> p h c", c=HEAD_STRIDE[j.i])
                nc.vector.tensor_reduce(mx[:, j.par, 0:j.heads], src[:, 0:j.heads, 0:j.keys], AX_X, ALU.max
                                        ).then_inc(mx_ready, 1)
                dve.wait_ge(mx_ready, j.number + 1)
                nc.vector.tensor_scalar(nb[:, j.par, 0:j.heads], mx[:, j.par, 0:j.heads], -SCALE, P_SHIFT,
                                        ALU.mult, ALU.add).then_inc(nb_ready, 1)

            def low_parts(j):
                for c in range(j.chunks):
                    dve.wait_ge(hi_ready[c], j.chunk_number(c) + 1)
                    n = (min(4 * c + 4, j.blocks) - 4 * c) * P
                    cols = slice(512 * c, 512 * c + n)
                    nc.vector.tensor_tensor(pt_lo[:, j.par, cols], ptb[:, c, 0:n], pt_hi[:, j.par, cols],
                                            ALU.subtract).then_inc(lo_ready[c], 1)

            def output(b, i, g):
                gn = 4 * tile(b, i) + g
                if not (isinstance(gn, int) and gn == 0):
                    dve.wait_ge(att_ready, gn)
                dve.wait_ge(olo_ready, gn + 1)
                nc.vector.reciprocal(rinv[:, :], rowsum[:, i % 2, bass.ds(GROUP * g, GROUP)]).then_inc(rinv_ready, 1)
                src = oacc[:, bass.ds((g % 2) * GROUP * 2 * D, GROUP * 2 * D)].rearrange("p (k c) -> p k c", c=2 * D)
                nc.vector.tensor_tensor(olo[:, :, :], src[:, :, 0:D], olo[:, :, :], ALU.add).then_inc(osum_ready, 1)
                dve.wait_ge(rinv_ready, gn + 1)
                dve.wait_ge(osum_ready, gn + 1)
                if not (isinstance(gn, int) and gn == 0):
                    dve.wait_ge(x1_ready, gn)
                nc.vector.tensor_tensor(att[:, :, :], olo[:, :, :], rinv[:, :].unsqueeze(2).to_broadcast([P, GROUP, D]),
                                        ALU.mult).then_inc(att_ready, 1)

            def take_second_half(u, dst):
                dve.wait_ge(slot_filled, u.filled)
                nc.vector.tensor_copy(dst, slot16[:, u.slot, 8:16, :]).then_inc(slot_released[u.slot], 1)

            def moments(k, t, src, s_stats, s_mv, s_rs):
                if not (isinstance(t, int) and t == 0):
                    dve.wait_ge(s_rs, 3 * t)
                for half in range(2):
                    nc.vector.bn_stats(stats[:, k, 6 * half:6 * half + 6], src[:, 512 * half:512 * half + 512]
                                       ).then_inc(s_stats, 1)
                dve_wait_apart(k, s_stats, 2 * t + 2)
                nc.vector.bn_aggr(mv[:, k, :], stats[:, k, :]).then_inc(s_mv, 1)

            def q_moments(t, i, n_in):
                dve.wait_ge(x_in[i % 4], 16 * n_in)
                moments(0, t, ring[:, i % NT, :], q_stats, q_mv, q_rs)

            def q_split(t):
                dve.wait_ge(q_hi, t + 1)
                nc.vector.tensor_tensor(q16[:, :, D:2 * D], norm32[:, :].rearrange("p (h d) -> p h d", d=D),
                                        q16[:, :, 0:D], ALU.subtract).then_inc(q_lo, 1)

            def c_split(t, i):
                dve.wait_ge(c_hi, t + 1)
                nc.vector.tensor_tensor(c16[:, i % 2, :, D:2 * D], cin[:, i % 2, :].rearrange("p (h d) -> p h d", d=D),
                                        c16[:, i % 2, :, 0:D], ALU.subtract).then_inc(c_lo, 1)

            def y_moments(t, i):
                dve.wait_ge(x1_ready, 4 * t + 4)
                moments(1, t, ring[:, i % NT, :], y_stats, y_mv, y_rs)

            def y_split(t):
                dve.wait_ge(y_hi, t + 1)
                nc.vector.tensor_tensor(y16[:, 1, :, :], norm32[:, :].rearrange("p (k c) -> p k c", c=P),
                                        y16[:, 0, :, :], ALU.subtract).then_inc(y_lo, 1)

            def result(u, t, i):
                dve.wait_ge(slot_filled, u.filled)
                dve.wait_ge(xb_ready, t + 1)
                nc.vector.tensor_tensor(xb[:, i % 2, :], slot[:, u.slot, :], xb[:, i % 2, :], ALU.add
                                        ).then_inc(slot_released[u.slot], 2)

            steps = [0]

            def bias_link(ins):
                steps[0] += 1
                ins.then_inc(bias_step, 1)
                dve.wait_ge(bias_step, steps[0])

            dve.wait_ge(coef_tanh, 1)
            bias_link(nc.vector.tensor_scalar(coef, coef, 0.5, 0.5, ALU.mult, ALU.add))
            bias_link(nc.vector.tensor_tensor(coef, coef, small[:, 0:4], ALU.mult))
            bias_link(nc.vector.tensor_scalar(coef, coef, small[:, 12:13], 0.5, ALU.mult, ALU.mult))
            bias_link(nc.vector.tensor_tensor(bits[:, 0, :], bits[:, 0, :], bits[:, 1, :], ALU.subtract))
            bit = bits[:, 0, :].rearrange("p (j n) -> p j n", n=NBITS)
            bias_link(nc.vector.tensor_scalar(bvec[:, :], bit[:, :, 0], small[:, 4:5], None, ALU.mult))
            for n in range(1, NBITS):
                bias_link(nc.vector.scalar_tensor_tensor(bvec[:, :], bit[:, :, n], small[:, 4 + n:5 + n], bvec[:, :],
                                                         ALU.mult, ALU.add))
            levels = float(2 ** NBITS - 1)
            bias_link(nc.vector.tensor_scalar(bvec[:, :], bvec[:, :], 1.0, -1.0, ALU.min, ALU.max))
            bias_link(nc.vector.tensor_scalar(bvec[:, :], bvec[:, :], levels, ROUND, ALU.mult, ALU.add))
            bias_link(nc.vector.tensor_scalar(bvec[:, :], bvec[:, :], ROUND, 1.0 / levels, ALU.subtract, ALU.mult))
            bias_link(nc.vector.tensor_scalar(bvec[:, :], bvec[:, :], small[:, 13:14], None, ALU.mult))
            assert steps[0] == 12
            dve.wait_ge(pool_const, 10)
            for j in range(8):
                ins = nc.vector.tensor_scalar(bdiag[:, j, :], id32[:, :], bvec[:, j:j + 1], None, ALU.mult)
                if j >= 2:
                    ins.then_inc(bias_step, 1)
            dve.wait_ge(slot_filled, 1)
            nc.vector.tensor_copy(bias_row[:, :].rearrange("p (q j) -> p j q", j=8)[:, 4:8, :],
                                  slot[:, 0, 512:1024].rearrange("p (j q) -> p j q", j=4)
                                  ).then_inc(slot_released[0], 1)
            q_moments(0, 0, 1)
            c_split(0, 0)
            q_split(0)
            take_second_half(Use(1), qt[:, 0, 8:16, :])
            take_second_half(Use(2), kt16[:, 0, 8:16, :])
            q_moments(1, 1, 1)
            c_split(1, 1)
            q_split(1)
            maxima(Job(0, 0, 0))

            def section(b, i):
                first = isinstance(b, int) and b == 0
                t = tile(b, i)

                def mid():
                    take_second_half(use(b, "QT", i), qt[:, (i + 1) % 2, 8:16, :])
                    take_second_half(use(b, "KT", i), kt16[:, (i + 1) % NT, 8:16, :])
                    if not (first and i < LAG):
                        take_second_half(use(b, "YT", i), yt[:, 1, :, :])

                def prepare():
                    q_moments(t + 2, i + 2, (i + 2) // 4 + 1 + 2 * b)
                    if not (first and i < LAG - 1):
                        y_moments(t - LAG + 1, i - LAG + 1)
                    c_split(t + 2, i + 2)
                    q_split(t + 2)
                    if not (first and i < LAG - 1):
                        y_split(t - LAG + 1)

                def weights(o):
                    for n in range(o * NWCH, (o + 1) * NWCH):
                        c = n % NWCH
                        dst = w32[:, c * WCH:(c + 1) * WCH]
                        diff = wp[:, n % 2].rearrange("p (k n) -> p k n", n=NBITS)
                        dve.wait_ge(d_ready, n + 1)
                        if c == 0 and o > 0:
                            dve.wait_ge(w_lo, o)
                        nc.vector.tensor_scalar(dst, diff[:, :, 0], coef[:, 0:1], None, ALU.mult
                                                ).then_inc(w_step, 1)
                        for k in range(1, NBITS):
                            dve.wait_ge(w_step, NBITS * n + k)
                            nc.vector.scalar_tensor_tensor(dst, diff[:, :, k], coef[:, k:k + 1], dst,
                                                           ALU.mult, ALU.add).then_inc(w_step, 1)
                    dve.wait_ge(w_hi, o + 1)
                    nc.vector.tensor_tensor(y16[:, 1, :, :], w32.rearrange("p (k c) -> p k c", c=P),
                                            y16[:, 0, :, :], ALU.subtract).then_inc(w_lo, 1)

                def ffn():
                    if not (first and i < LAG):
                        result(use(b, "FFN", i), t - LAG, i - LAG)

                maxima(Job(b, i, 1))
                low_parts(Job(b, i, 0))

                def body(g):
                    for s in range(1, JPG[i] + 1):
                        j = Job(b, i, s, g)
                        if not isinstance(g, int) or JPG[i] * g + s + 1 < JOBS[i]:
                            maxima(j.next())
                        low_parts(j)
                    output(b, i, g)
                group_loop(dve, i, body)
                if i < NT - 1:
                    mid()
                for q in range(3 * JPG[i] + 1, JOBS[i]):
                    j = Job(b, i, q)
                    if q + 1 < JOBS[i]:
                        maxima(j.next())
                    low_parts(j)
                if i < NT - 1:
                    maxima(first_job(b, i + 1))
                    prepare()
                    if first and i < 4:
                        for o in (2 * i, 2 * i + 1):
                            weights(o)
                            take_second_half(use(b, "WT", o), wt[:, 1, :, o * P:(o + 1) * P])
                    ffn()
                    output(b, i, 3)
                else:
                    mid()
                    output(b, i, 3)
                    prepare()
                    ffn()
                    maxima(first_job(b, i + 1))

            batches(dve, section)
            for k in range(LAG):
                t = B * NT - LAG + k
                if k < LAG - 1:
                    y_moments(t + 1, t + 1)
                take_second_half(Use(END_USE + 2 * k), yt[:, 1, :, :])
                if k < LAG - 1:
                    y_split(t + 1)
                result(Use(END_USE + 2 * k + 1), t, t)

        @block.gpsimd
        def _(pool):
            def deviation(k, t, s_mv, s_rs):
                pool_wait_apart(2 + 3 * k, s_mv, t + 1)
                nc.gpsimd.tensor_scalar(rstd[:, k, 0:1], mv[:, k, 1:2], EPS, None, ALU.add).then_inc(s_rs, 1)
                pool.wait_ge(s_rs, 3 * t + 1)
                nc.gpsimd.tensor_tensor(rstd[:, k, 1:2], rstd[:, k, 0:1], half_neg[:, :], ALU.pow).then_inc(s_rs, 1)
                pool_wait_apart(3 + 3 * k, s_rs, 3 * t + 2)
                nc.gpsimd.tensor_scalar(rstd[:, k, 2:3], mv[:, k, 0:1], rstd[:, k, 1:2], -1.0, ALU.mult, ALU.mult
                                        ).then_inc(s_rs, 1)

            def normalise(k, t, src, last_reader, done):
                if last_reader is not None:
                    pool.wait_ge(*last_reader)
                pool_wait_apart(4 + 3 * k, (q_rs, y_rs)[k], 3 * t + 3)
                nc.gpsimd.tensor_scalar(norm32[:, :], src, rstd[:, k, 1:2], rstd[:, k, 2:3], ALU.mult, ALU.add
                                        ).then_inc(done, 1)

            def add_attention(b, i, g, n_in):
                gn = 4 * tile(b, i) + g
                pool.wait_ge(att_ready, gn + 1)
                dst = ring[:, i % NT, bass.ds(GROUP * D * g, GROUP * D)]
                nc.gpsimd.tensor_tensor(dst, dst, att[:, :, :].rearrange("p h d -> p (h d)"), ALU.add
                                        ).then_inc(x1_ready, 1)

            def add_bias(t, i, n_out):
                if n_out is not None:
                    pool.wait_ge(out_done[i % 2], 16 * n_out)
                nc.gpsimd.tensor_tensor(xb[:, i % 2, :], ring[:, i % NT, :], bias_row[:, :], ALU.add
                                        ).then_inc(xb_ready, 1)

            nc.gpsimd.memset(id32[:, :], 0.0).then_inc(pool_const, 1)
            nc.gpsimd.memset(id16[:, :], 0.0).then_inc(pool_const, 1)
            nc.gpsimd.memset(idb[:, :], 0.0).then_inc(pool_const, 1)
            nc.gpsimd.memset(maskb[:, :], 0.0).then_inc(pool_const, 1)
            nc.gpsimd.memset(ones32[:, :], 1.0).then_inc(pool_const, 1)
            nc.gpsimd.memset(half_neg[:, :], -0.5).then_inc(pool_const, 1)
            pool.wait_ge(pool_const, 6)
            for m in (id32, id16, idb):
                nc.gpsimd.affine_select(out=m[:, :], in_=m[:, :], compare_op=ALU.not_equal, fill=1.0, base=0,
                                        pattern=[[-1, P]], channel_multiplier=1).then_inc(pool_const, 1)
            nc.gpsimd.affine_select(out=maskb[:, :], in_=maskb[:, :], compare_op=ALU.is_ge, fill=MASKED, base=0,
                                    pattern=[[-1, P]], channel_multiplier=1).then_inc(pool_const, 1)
            deviation(0, 0, q_mv, q_rs)
            normalise(0, 0, ring[:, 0, :], (slot_filled, 1), q_norm)
            deviation(0, 1, q_mv, q_rs)
            normalise(0, 1, ring[:, 1, :], (q_lo, 1), q_norm)

            def section(b, i):
                first = isinstance(b, int) and b == 0
                t = tile(b, i)

                def prepare():
                    deviation(0, t + 2, q_mv, q_rs)
                    normalise(0, t + 2, ring[:, (i + 2) % NT, :],
                              (q_lo, t + 2) if first and i < LAG else (y_lo, t - LAG + 1), q_norm)
                    if not (first and i < LAG - 1):
                        u = t - LAG + 1
                        deviation(1, u, y_mv, y_rs)
                        normalise(1, u, ring[:, (i - LAG + 1) % NT, :], (q_lo, t + 3), y_norm)
                        n_out = 4 * b + (i - LAG + 1) // 2
                        add_bias(u, i - LAG + 1, n_out if not (first and i < LAG + 1) else None)

                group_loop(pool, i, lambda g: add_attention(b, i, g, None))
                if i < NT - 1:
                    prepare()
                    if first and i < 4:
                        for n in range(2 * i * NWCH, (2 * i + 2) * NWCH):
                            pool.wait_ge(th_ready, n + 1)
                            nc.gpsimd.tensor_tensor(wp[:, n % 2], wp[:, n % 2], wn[:, n % 2], ALU.subtract
                                                    ).then_inc(d_ready, 1)
                    add_attention(b, i, 3, None)
                else:
                    add_attention(b, i, 3, None)
                    prepare()

            batches(pool, section)
            for k in range(LAG - 1):
                t = B * NT - LAG + k + 1
                deviation(1, t, y_mv, y_rs)
                normalise(1, t, ring[:, t % NT, :], (y_lo, t), y_norm)
                add_bias(t, t, t // 2)


END_USE = USE_LATER_BASE + (B - 1) * len(USE_LATER) + 1

_INS = ['x', 'ctx_2048', 'L0_ffn_pweight', 'L0_ffn_nweight', 'L0_ffn_exps', 'L0_ffn_bexps', 'L0_ffn_mask_weight',
        'L0_ffn_scale', 'L0_ffn_pbias', 'L0_ffn_nbias', 'L0_ffn_biasscale']


def kernel(**inputs):
    import numpy as _np
    import concourse.bacc as _bacc
    from concourse.bass_utils import run_bass_kernel_spmd as _run

    nc = _bacc.Bacc("TRN2", target_bir_lowering=False, num_devices=1)
    arrays, args = {}, []
    for name in _INS:
        a = _np.ascontiguousarray(inputs[name])
        arrays[f"in_{name}_dram"] = a
        args.append(nc.dram_tensor(f"in_{name}_dram", a.shape, mybir.dt.from_np(a.dtype), kind="ExternalInput").ap())
    args.append(nc.dram_tensor("out_0_dram", (B, SEQ, DM), F32, kind="ExternalOutput").ap())
    build(nc, *args)
    r = _run(nc, [arrays], core_ids=[0])
    return r.results[0]["out_0_dram"]
```

```python
import math
from contextlib import ExitStack

import concourse.bass as bass
from concourse import mybir

ALU = mybir.AluOpType
ACT = mybir.ActivationFunctionType
AX_X = mybir.AxisListType.X
F32 = mybir.dt.float32
F16 = mybir.dt.float16
BF16 = mybir.dt.bfloat16

P = 128
B, SEQ, DM = 4, 1024, 1024
NT = SEQ // P
H, D = 16, 64
KT_N = DM // P
NBITS = 4
EPS = 1e-5
SCALE = D ** -0.5
LAG = 5
GROUP = 4
P_SHIFT = 10 * math.log(2)
MASKED = -1e30
ROUND = 1.5 * 2 ** 23

HPJ = [4, 4, 2, 2, 1, 1, 1, 1]
JPG = [GROUP // h for h in HPJ]
JOBS = [H // h for h in HPJ]
JOB0 = [sum(JOBS[:i]) for i in range(NT + 1)]
HEAD_STRIDE = [128, 256, 512, 512, 1024, 1024, 1024, 1024]


def has_linear(b, i):
    return not (isinstance(b, int) and b == 0 and i < LAG)


def has_weights(b, i):
    return isinstance(b, int) and b == 0 and i < 4


def weight_tiles_after(i, g):
    k = 4 * i + g
    return ([(k - 3) // 2] if k % 2 and k >= 3 else []) + ([7] if k == 15 else [])


def looped(i):
    return max(3 * JPG[i], JOBS[i] - 2)


def uses_of(first):
    b = 0 if first else 1
    seq = []

    def scores_ahead(i, steps):
        return [("S", *ahead(i, q)) for q in steps if ahead(i, q)]

    for i in range(NT):
        seq += scores_ahead(i, range(2)) + [("QT", i)]
        seq += [("KT", i)] if i < NT - 1 else []
        seq += [("YT", i)] if has_linear(b, i) else []
        for g in range(3):
            seq += scores_ahead(i, steps_of_group(i, g))
            seq += [("WT", o) for o in weight_tiles_after(i, g)] if has_weights(b, i) else []
        seq += scores_ahead(i, range(3 * JPG[i] + 2, JOBS[i]))
        if i < NT - 1:
            seq += [("WT", o) for o in weight_tiles_after(i, 3)] if has_weights(b, i) else []
            seq += [("FFN", i)] if has_linear(b, i) else []
        else:
            seq += [("KT", i), ("S", NT, 0), ("S", NT, 1)] + ([("FFN", i)] if has_linear(b, i) else [])
    return {u: n for n, u in enumerate(seq)}


def steps_of_group(i, g):
    return range(JPG[i] * g + 2, JPG[i] * g + JPG[i] + 2)


def ahead(i, q):
    if q + 2 < JOBS[i]:
        return i, q + 2
    return (i + 1, q + 2 - JOBS[i]) if q < JOBS[i] and i < NT - 1 else None


USE_FIRST, USE_LATER = uses_of(True), uses_of(False)
USE_BASE = 5
USE_LATER_BASE = USE_BASE + len(USE_FIRST)


class Use:

    def __init__(self, const, run=0):
        self.const, self.run = const, run
        self.slot = const % 2
        self.filled = const + run + 1
        self.released = const - const % 2 + 2 + run
        self.free = const - const % 2 + run
        self.wait_free = not (isinstance(run, int) and const + run < 2)


def use(b, *key):
    if key[:2] == ("S", 0) and key[2] < 2:
        return Use(USE_BASE - 2 + key[2]) if isinstance(b, int) and b == 0 else use_before(b, "S", NT, key[2])
    if isinstance(b, int) and b == 0:
        return Use(USE_BASE + USE_FIRST[key])
    return Use(USE_LATER_BASE - len(USE_LATER) + USE_LATER[key], len(USE_LATER) * b)


def use_before(b, *key):
    return Use(USE_LATER_BASE - 2 * len(USE_LATER) + USE_LATER[key], len(USE_LATER) * b)


class Job:

    def __init__(self, b, i, s, g=0):
        self.b, self.i, self.s, self.g = b, i, s, g
        static = isinstance(g, int)
        q = JPG[i] * g + s
        self.heads = HPJ[i]
        self.blocks = self.heads * (i + 1)
        self.chunks = (self.blocks + 3) // 4
        self.keys = (i + 1) * P
        self.head0 = GROUP * g + HPJ[i] * s
        self.number = b * JOB0[NT] + JOB0[i] + q
        self.par = (q if static else s) % 2
        self.number1 = b * (JOB0[NT] - JOBS[0]) + JOB0[i] - JOBS[0] + q
        if static:
            self.use = use(b, "S", i, q) if q < JOBS[i] else None
        else:
            base = use(b, "S", i, 4)
            self.use = Use(base.const + s - 4, base.run + JPG[i] * g)

    def chunk_number(self, c):
        return self.number1 if c else self.number


def next_job(b, i, q):
    if i < NT - 1:
        return Job(b, i + 1, q)
    j = Job(b, 0, q)
    j.number = b * JOB0[NT] + JOB0[NT] + q
    j.use = use(b, "S", NT, q)
    return j


def job_ahead(b, i, s, g=0):
    if not isinstance(g, int):
        return Job(b, i, s + 2, g)
    q = JPG[i] * g + s
    if ahead(i, q) is None:
        return None
    return Job(b, i, s + 2, g) if q + 2 < JOBS[i] else next_job(b, i, q + 2 - JOBS[i])


def group_loop(eng, b, i, body):
    if JPG[i] == 1 or has_weights(b, i):
        for g in range(3):
            body(g)
    else:
        alike = 3 if JPG[i] > 2 else 2
        with eng.Fori(0, alike) as g:
            body(g)
        for g in range(alike, 3):
            body(g)


def batches(eng, section):
    for i in range(NT):
        section(0, i)
    with eng.Fori(1, B) as b:
        for i in range(NT):
            section(b, i)


def build(nc, x, ctx_in, pweight, nweight, exps, bexps, mask_weight, scale, pbias, nbias, biasscale, out):
    x_t = x.rearrange("b (i p) d -> (b i) p d", p=P)
    c_t = ctx_in.rearrange("b (i p) d -> (b i) p d", p=P)
    out_t = out.rearrange("b (i p) d -> (b i) p d", p=P)
    WCH = 256
    NWCH = DM // WCH
    pw_t = pweight.rearrange("(o p) (c k) n -> o c p (k n)", p=P, k=WCH)
    nw_t = nweight.rearrange("(o p) (c k) n -> o c p (k n)", p=P, k=WCH)

    with ExitStack() as stack:
        def sb(name, shape, dt):
            return stack.enter_context(nc.sbuf_tensor(name, shape, dt))

        def sem(name):
            return stack.enter_context(nc.semaphore(name))

        wt = sb("wt", [P, 2, KT_N, DM], F16)
        v16 = sb("v16", [P, NT, H, 2 * D], F16)
        kt16 = sb("kt16", [P, NT, H, P], F16)
        ring = sb("ring", [P, NT, DM], F32)
        cin = sb("cin", [P, DM], F32)
        c16 = sb("c16", [P, 2, H, 2 * D], F16)
        norm32 = sb("norm32", [P, DM], F32)
        q16 = sb("q16", [P, H, 2 * D], F16)
        qt = sb("qt", [P, 2, H, P], F16)
        qs = sb("qs", [P, 2, H, P], F16)
        p32 = sb("p32", [P, 2, 8 * P], F32)
        pt_hi = sb("pt_hi", [P, 2, 8 * P], F16)
        pt_lo = sb("pt_lo", [P, 2, 8 * P], F16)
        osb = sb("osb", [P, GROUP, 2 * D], F32)
        att = sb("att", [P, GROUP, D], F32)
        y16 = sb("y16", [P, 2, KT_N, P], F16)
        yt = sb("yt", [P, 2, KT_N, P], F16)
        xb = sb("xb", [P, 2, DM], F32)
        bias_row = sb("bias_row", [P, DM], F32)
        pairs = [(xb[:, 0, :], xb[:, 1, :])] + [
            tuple(m[:, k].rearrange("p h c -> p (h c)").bitcast(F32) for m, k in two)
            for two in (((v16, 5), (v16, 6)), ((v16, 7), (kt16, 7)), ((kt16, 5), (kt16, 6)))]
        w32 = yt[:, :, :, :].bitcast(F32).rearrange("p a b c -> p (a b c)")
        ones32 = y16[:, 0, 0:2, :].bitcast(F32).rearrange("p a b -> p (a b)")
        end_yt = [yt, v16[:, 4].rearrange("p (a k) c -> p a k c", a=2)]
        id32 = sb("id32", [P, P], F32)
        id16 = sb("id16", [P, P], F16)
        idb = sb("idb", [P, P], BF16)
        maskb = sb("maskb", [P, P], BF16)
        half_neg = sb("half_neg", [P, 1], F32)
        gate = sb("gate", [P, 8], F32)
        mx = sb("mx", [P, 2, GROUP], F32)
        nb = sb("nb", [P, 2, GROUP], F32)
        rowsum = sb("rowsum", [P, 2, H], F32)
        rinv = sb("rinv", [P, GROUP], F32)
        stats = sb("stats", [P, 2, 12], F32)
        mv = sb("mv", [P, 2, 2], F32)
        rstd = sb("rstd", [P, 2, 3], F32)
        small = sb("small", [P, 18], F32)
        coef = small[:, 14:18]
        bits = y16[:, 1, 0, :].bitcast(F32).rearrange("p (a n) -> p a n", a=2)
        bvec = sb("bvec", [P, 8], F32)
        bdiag = norm32[:, :].rearrange("p (j q) -> p j q", j=8)

        slot = stack.enter_context(nc.psum_tensor("slot", [P, 2, 1024], F32))
        ptb = stack.enter_context(nc.psum_tensor("ptb", [P, 2, 512], F32))
        oacc = stack.enter_context(nc.psum_tensor("oacc", [P, 8 * 2 * D], F32))
        slot16 = slot[:, :, :].bitcast(F16).rearrange("p s (k c) -> p s k c", c=P)

        x_in = [sem(f"x_in{r}") for r in range(4)]
        c_in = [sem(f"c_in{r}") for r in range(2)]
        v_in = [sem(f"v_in{r}") for r in range(2)]
        qs_in = [sem(f"qs_in{r}") for r in range(2)]
        w_in = [sem(f"w_in{r}") for r in range(4)]
        out_done = [sem(f"out_done{r}") for r in range(2)]
        small_in = sem("small_in")
        slot_filled = sem("slot_filled")
        slot_released = [sem(f"slot_released{r}") for r in range(2)]
        mx_ready = sem("mx_ready")
        nb_ready = sem("nb_ready")
        pt_filled = [sem(f"pt_filled{c}") for c in range(2)]
        hi_ready = [sem(f"hi_ready{c}") for c in range(2)]
        lo_ready = [sem(f"lo_ready{c}") for c in range(2)]
        pv_done = sem("pv_done")
        rinv_ready = sem("rinv_ready")
        osb_ready = sem("osb_ready")
        osb_added = sem("osb_added")
        att_ready = sem("att_ready")
        x1_ready = sem("x1_ready")
        q_stats, q_mv, q_rs, q_norm, q_hi, q_lo = (sem("q_" + n) for n in ("stats", "mv", "rs", "norm", "hi", "lo"))
        c_hi, c_lo = sem("c_hi"), sem("c_lo")
        y_stats, y_mv, y_rs, y_norm, y_hi, y_lo = (sem("y_" + n) for n in ("stats", "mv", "rs", "norm", "hi", "lo"))
        xb_ready = sem("xb_ready")
        pool_const = sem("pool_const")
        th_ready, d_ready, w_step, w_hi, w_lo = (sem("w_" + n) for n in ("tanh", "diff", "step", "hi", "lo"))
        coef_tanh = sem("coef_tanh")
        coef_step = sem("coef_step")
        bias_step = sem("bias_step")

        def tile(b, i):
            return NT * b + i

        def dve_wait_apart(column, s, value):
            nc.vector.wait_ge(s, value)
            nc.vector.memset(gate[:, column:column + 1], 0.0)

        def pool_wait_apart(column, s, value):
            nc.gpsimd.wait_ge(s, value)
            nc.gpsimd.tensor_tensor(gate[:, column:column + 1], half_neg[:, :], half_neg[:, :], ALU.add)

        block = stack.enter_context(nc.Block())

        @block.sync
        def _(sp):
            def load_x(b, k, t):
                if not (isinstance(t, int) and t < NT):
                    sp.wait_ge(xb_ready, t - NT + 1)
                src = x_t[t] if isinstance(t, int) else x_t[bass.ds(t % (B * NT), 1)].rearrange("a p d -> (a p) d")
                sp.dma_start(ring[:, k % NT, :], src).then_inc(x_in[k % 4], 16)

            def load_c(b, k, t):
                if not (isinstance(t, int) and t == 0):
                    sp.wait_ge(c_lo, t)
                src = c_t[t] if isinstance(t, int) else c_t[bass.ds(t % (B * NT), 1)].rearrange("a p d -> (a p) d")
                sp.dma_start(cin[:, :], src).then_inc(c_in[k % 2], 16)

            def keep_v(t, i, pv):
                sp.wait_ge(c_lo, t + 1)
                if pv is not None:
                    sp.wait_ge(pv_done, pv)
                sp.dma_start(v16[:, i % NT], c16[:, i % 2]).then_inc(v_in[i % 2], 16)

            def swap(u, i):
                sp.wait_ge(slot_released[u.slot], u.released)
                sp.dma_start(qs[0:D, i % 2], qt[D:P, i % 2]).then_inc(qs_in[i % 2], 16)
                sp.dma_start(qs[D:P, i % 2], qt[0:D, i % 2]).then_inc(qs_in[i % 2], 16)

            def load_w(n):
                if n >= 4:
                    sp.wait_ge(w_step, NBITS * (n - 3))
                sp.dma_start(pairs[n % 4][0], pw_t[n // NWCH, n % NWCH]).then_inc(w_in[n % 4], 16)
                sp.dma_start(pairs[n % 4][1], nw_t[n // NWCH, n % NWCH]).then_inc(w_in[n % 4], 16)

            for at, src in ((0, exps), (4, bexps), (8, mask_weight), (12, scale), (13, biasscale)):
                n = src.shape[0]
                sp.dma_start(small[:, at:at + n], src.rearrange("(a n) -> a n", a=1).to_broadcast([P, n])
                             ).then_inc(small_in, 16)
            for k, src in enumerate((pbias, nbias)):
                sp.dma_start(bits[:, k, :], src.rearrange("(p j) n -> p (j n)", p=P)).then_inc(small_in, 16)
            load_x(0, 0, 0)
            load_c(0, 0, 0)
            load_x(0, 1, 1)
            for n in range(4):
                load_w(n)
            load_x(0, 2, 2)
            load_c(0, 1, 1)
            swap(Use(1), 0)
            keep_v(0, 0, None)

            def section(b, i):
                t = tile(b, i)
                load_x(b, i + 3, t + 3)
                load_c(b, i + 2, t + 2)
                if isinstance(b, int) and b == 0 and i == 4:
                    sp.wait_ge(w_step, NBITS * 32)
                if i < NT - 1:
                    keep_v(t + 1, i + 1, None)
                swap(use(b, "QT", i), i + 1)
                if i == NT - 1:
                    keep_v(t + 1, i + 1, b * JOB0[NT] + JOB0[NT])
                if has_weights(b, i):
                    for n in range(max(8 * i + 2, 4), min(8 * i + 10, 32)):
                        load_w(n)
                if has_linear(b, i):
                    store(use(b, "FFN", i), t - LAG, i - LAG)

            def store(u, t, k):
                sp.wait_ge(slot_released[u.slot], u.released)
                dst = out_t[t] if isinstance(t, int) else out_t[bass.ds(t, 1)].rearrange("a p d -> (a p) d")
                sp.dma_start(dst, xb[:, k % 2, :]).then_inc(out_done[k % 2], 16)

            batches(sp, section)
            for k in range(LAG):
                t = B * NT - LAG + k
                store(end_linear(k), t, t)
            for r in range(2):
                sp.wait_ge(out_done[r], 16 * B * NT // 2)

        @block.tensor
        def _(pe):
            def take(u):
                if u.wait_free:
                    pe.wait_ge(slot_released[u.slot], u.free)

            def scores(j):
                i = j.i
                take(j.use)
                for hh in range(j.heads):
                    h = j.head0 + hh
                    base = hh * HEAD_STRIDE[i]
                    for w in range((i + 4) // 4):
                        blocks = min(4, i + 1 - 4 * w)
                        dst = slot[:, j.use.slot, base + 512 * w:base + 512 * w + blocks * P]
                        keys = kt16[:, 4 * w:4 * w + blocks, h, :]
                        diagonal = 4 * w + blocks == i + 1
                        pe.matmul(dst, qt[:, i % 2, h, :], keys, start=True, stop=False, skip_group_check=True)
                        last = pe.matmul(dst, qs[:, i % 2, h, :], keys, start=False, stop=not diagonal,
                                         skip_group_check=True)
                        if diagonal:
                            dst = slot[:, j.use.slot, base + i * P:base + (i + 1) * P]
                            last = pe.matmul(dst, idb[:, :], maskb[:, :], start=False, stop=True,
                                             skip_group_check=True)
                last.then_inc(slot_filled, 1)

            def scores_of_new_tile(b, i, j):
                for name in ("QT", "KT"):
                    u = use(b, name, i)
                    if u.slot != j.use.slot:
                        pe.wait_ge(slot_released[u.slot], u.released)
                n = (i + 1) // 2 + 1 + 4 * b
                pe.wait_ge(qs_in[(i + 1) % 2], 32 * n)
                scores(j)

            def transpose_p(j):
                pe.wait_ge(slot_released[j.use.slot], j.use.released)
                for c in range(j.chunks):
                    n = j.chunk_number(c)
                    if not (isinstance(n, int) and n == 0):
                        pe.wait_ge(lo_ready[c], n)
                    for k in range(4 * c, min(4 * c + 4, j.blocks)):
                        last = pe.transpose(ptb[:, c, (k - 4 * c) * P:(k - 4 * c + 1) * P],
                                            p32[:, j.par, k * P:(k + 1) * P], id32[:, :])
                    last.then_inc(pt_filled[c], 1)

            def values(j, g):
                i = j.i
                first_of_group = (j.s % JPG[i] == 0) if isinstance(j.g, int) else j.s == 0
                gn = 4 * tile(j.b, i) + g
                if first_of_group and not (isinstance(gn, int) and gn < 2):
                    pe.wait_ge(osb_ready, gn - 1)
                for c in range(j.chunks):
                    pe.wait_ge(lo_ready[c], j.chunk_number(c) + 1)
                for hh in range(j.heads):
                    h = j.head0 + hh
                    k0 = (HPJ[i] * j.s + hh) % GROUP
                    at = (g % 2) * (GROUP * 2 * D) + k0 * 2 * D
                    for blk in range(i + 1):
                        k = hh * (i + 1) + blk
                        cols = slice(k * P, (k + 1) * P)
                        pe.matmul(oacc[:, bass.ds(at, 2 * D)], pt_hi[:, j.par, cols], v16[:, blk, h, :],
                                  start=blk == 0, stop=False, skip_group_check=True)
                        last = pe.matmul(oacc[:, bass.ds(at, D)], pt_lo[:, j.par, cols], v16[:, blk, h, 0:D],
                                         start=False, stop=blk == i, skip_group_check=True)
                last.then_inc(pv_done, 1)

            def turn(u, src):
                take(u)
                for k in range(16):
                    last = pe.transpose(slot16[:, u.slot, k, :], src(k), id16[:, :])
                last.then_inc(slot_filled, 1)

            def turn_q(u, t):
                pe.wait_ge(q_lo, t + 1)
                turn(u, lambda k: q16[:, k, :])

            def turn_k(u, t, i):
                pe.wait_ge(c_lo, t + 1)
                turn(u, lambda k: c16[:, i % 2, k, :])

            def turn_y(u, t):
                pe.wait_ge(y_lo, t + 1)
                turn(u, lambda k: y16[:, k // KT_N, k % KT_N, :])

            def linear(u, turned, yt):
                take(u)
                if turned.slot != u.slot:
                    pe.wait_ge(slot_released[turned.slot], turned.released)
                terms = ((0, 0), (1, 0), (0, 1))
                for half in range(2):
                    for n, (a, c) in enumerate(terms):
                        for k in range(KT_N):
                            last = pe.matmul(slot[:, u.slot, half * 512:half * 512 + 512], yt[:, a, k, :],
                                             wt[:, c, k, half * 512:half * 512 + 512],
                                             start=n == 0 and k == 0, stop=n == len(terms) - 1 and k == KT_N - 1)
                last.then_inc(slot_filled, 1)

            pe.wait_ge(pool_const, 10)
            pe.wait_ge(bias_step, 18)
            for j in range(8):
                last = pe.matmul(slot[:, 0, j * P:(j + 1) * P], ones32[:, :], bdiag[:, j, :], start=True, stop=True)
            last.then_inc(slot_filled, 1)
            turn_q(Use(1), 0)
            turn_k(Use(2), 0, 0)
            for u in (Use(1), Use(2)):
                pe.wait_ge(slot_released[u.slot], u.released)
            pe.wait_ge(qs_in[0], 32)
            scores(Job(0, 0, 0))
            scores(Job(0, 0, 1))

            def section(b, i):
                t = tile(b, i)

                def step(j, g):
                    in_loop = not isinstance(j.g, int)
                    q = None if in_loop else JPG[i] * j.g + j.s
                    coming = job_ahead(b, i, j.s, j.g)
                    if coming and not in_loop and q + 2 == JOBS[i]:
                        scores_of_new_tile(b, i, coming)
                    elif coming:
                        scores(coming)
                    if in_loop or q >= 2:
                        values(Job(b, i, j.s - 2, j.g), g)
                    if in_loop or q < JOBS[i]:
                        transpose_p(j)

                def ffn():
                    if has_linear(b, i):
                        linear(use(b, "FFN", i), use(b, "YT", i), yt)

                def turn_weights(g):
                    for o in weight_tiles_after(i, g) if has_weights(b, i) else ():
                        pe.wait_ge(w_lo, o + 1)
                        turn(use(b, "WT", o), lambda k: y16[:, k // KT_N, k % KT_N, :])

                step(Job(b, i, 0), 0)
                step(Job(b, i, 1), 0)
                pe.wait_ge(v_in[i % 2], 16 * (i // 2 + 1 + 4 * b))
                turn_q(use(b, "QT", i), t + 1)
                if i < NT - 1:
                    turn_k(use(b, "KT", i), t + 1, i + 1)
                if has_linear(b, i):
                    turn_y(use(b, "YT", i), t - LAG)

                def body(g):
                    for s in range(2, JPG[i] + 2):
                        step(Job(b, i, s, g), g)
                    if isinstance(g, int):
                        turn_weights(g)
                group_loop(pe, b, i, body)
                if i == NT - 1:
                    turn_k(use(b, "KT", i), t + 1, i + 1)
                for q in range(3 * JPG[i] + 2, JOBS[i]):
                    step(Job(b, i, q), 3)
                if i == NT - 1:
                    scores_of_new_tile(b, i, next_job(b, i, 0))
                for q in range(looped(i), JOBS[i] - 1):
                    values(Job(b, i, q), 3)
                if i == NT - 1:
                    scores(next_job(b, i, 1))
                turn_weights(3)
                ffn()
                values(Job(b, i, JOBS[i] - 1), 3)

            batches(pe, section)
            turn_y(end_turned(0), B * NT - LAG)
            for k in range(LAG):
                if k < LAG - 1:
                    turn_y(end_turned(k + 1), B * NT - LAG + k + 1)
                linear(end_linear(k), end_turned(k), end_yt[k % 2])

        @block.scalar
        def _(act):
            def exponentials(j):
                act.wait_ge(mx_ready, j.number + 1)
                nc.scalar.activation(nb[:, j.par, 0:j.heads], mx[:, j.par, 0:j.heads], ACT.Copy, bias=P_SHIFT,
                                     scale=-SCALE).then_inc(nb_ready, 1)
                act.wait_ge(nb_ready, j.number + 1)
                for hh in range(j.heads):
                    base = hh * HEAD_STRIDE[j.i]
                    last = nc.scalar.activation(
                        p32[:, j.par, hh * j.keys:(hh + 1) * j.keys], slot[:, j.use.slot, base:base + j.keys],
                        ACT.Exp, bias=nb[:, j.par, hh:hh + 1], scale=SCALE,
                        accum_out=rowsum[:, j.i % 2, bass.ds(j.head0 + hh, 1)])
                last.then_inc(slot_released[j.use.slot], 2)

            def high_parts(j):
                if not (isinstance(j.number, int) and j.number < 2):
                    act.wait_ge(pv_done, j.number - 1)
                for c in range(j.chunks):
                    act.wait_ge(pt_filled[c], j.chunk_number(c) + 1)
                    n = (min(4 * c + 4, j.blocks) - 4 * c) * P
                    nc.scalar.copy(pt_hi[:, j.par, 512 * c:512 * c + n], ptb[:, c, 0:n]).then_inc(hi_ready[c], 1)

            def output(b, i, g, pv):
                gn = 4 * tile(b, i) + g
                if not (isinstance(gn, int) and gn == 0):
                    act.wait_ge(osb_added, gn)
                act.wait_ge(pv_done, pv)
                nc.scalar.copy(osb[:, :, :].rearrange("p k c -> p (k c)"),
                               oacc[:, bass.ds((g % 2) * GROUP * 2 * D, GROUP * 2 * D)]).then_inc(osb_ready, 1)

            def take_first_half(u, dst):
                act.wait_ge(slot_filled, u.filled)
                nc.scalar.copy(dst, slot16[:, u.slot, 0:8, :]).then_inc(slot_released[u.slot], 1)

            def q_split(t, i, turned):
                act.wait_ge(q_norm, t + 1)
                if turned is not None:
                    act.wait_ge(slot_filled, turned.filled)
                nc.scalar.copy(q16[:, :, 0:D], norm32[:, :].rearrange("p (h d) -> p h d", d=D)).then_inc(q_hi, 1)

            def c_split(t, i, turned, n_in):
                act.wait_ge(c_in[i % 2], 16 * n_in)
                if turned is not None:
                    act.wait_ge(slot_filled, turned.filled)
                    act.wait_ge(v_in[i % 2], 16 * (n_in - 1))
                nc.scalar.copy(c16[:, i % 2, :, 0:D], cin[:, :].rearrange("p (h d) -> p h d", d=D)
                               ).then_inc(c_hi, 1)

            def y_split(t, turned):
                act.wait_ge(y_norm, t + 1)
                if turned is not None:
                    act.wait_ge(slot_filled, turned.filled)
                nc.scalar.copy(y16[:, 0, :, :], norm32[:, :].rearrange("p (k c) -> p k c", c=P)).then_inc(y_hi, 1)

            act.wait_ge(small_in, 16 * 7)
            nc.scalar.activation(coef, small[:, 8:12], ACT.Tanh, scale=0.5).then_inc(coef_tanh, 1)
            c_split(0, 0, None, 1)
            q_split(0, 0, None)
            act.wait_ge(slot_filled, 1)
            nc.scalar.copy(bias_row[:, :].rearrange("p (q j) -> p j q", j=8)[:, 0:4, :],
                           slot[:, 0, 0:512].rearrange("p (j q) -> p j q", j=4)).then_inc(slot_released[0], 1)
            take_first_half(Use(1), qt[:, 0, 0:8, :])
            take_first_half(Use(2), kt16[:, 0, 0:8, :])
            c_split(1, 1, None, 1)
            q_split(1, 1, Use(1))
            exponentials(Job(0, 0, 0))
            exponentials(Job(0, 0, 1))

            def section(b, i):
                first = isinstance(b, int) and b == 0
                t = tile(b, i)
                jobs0 = b * JOB0[NT] + JOB0[i]

                def prepare():
                    if i > 0:
                        c_turned = use(b, "KT", i - 1)
                    else:
                        c_turned = Use(2) if first else use_before(b, "KT", NT - 1)
                    c_split(t + 2, i + 2, c_turned, (i + 2) // 2 + 1 + 4 * b)
                    q_split(t + 2, i + 2, use(b, "QT", i))
                    if has_linear(b, i + 1):
                        y_split(t - LAG + 1, None if not has_linear(b, i) else use(b, "YT", i))

                def weights_high(o):
                    act.wait_ge(w_step, NBITS * NWCH * (o + 1))
                    if o > 0:
                        act.wait_ge(slot_filled, use(0, "WT", o - 1).filled)
                    nc.scalar.copy(y16[:, 0, :, :], w32.rearrange("p (k c) -> p k c", c=P)).then_inc(w_hi, 1)

                def weights(g):
                    k = 4 * i + g
                    for n in (2 * k, 2 * k + 1):
                        act.wait_ge(w_in[n % 4], 32 * (n // 4 + 1))
                        for half in pairs[n % 4]:
                            last = nc.scalar.activation(half, half, ACT.Tanh, scale=0.5)
                        last.then_inc(th_ready, 1)
                    if k % 2 == 0 and k >= 2:
                        weights_high((k - 2) // 2)
                    for o in weight_tiles_after(i, g):
                        if o == 7:
                            weights_high(7)
                        take_first_half(use(b, "WT", o), wt[:, 0, :, o * P:(o + 1) * P])

                def step(j):
                    in_loop = not isinstance(j.g, int)
                    q = None if in_loop else JPG[i] * j.g + j.s
                    if in_loop or q < JOBS[i]:
                        high_parts(j)
                    if job_ahead(b, i, j.s, j.g):
                        exponentials(job_ahead(b, i, j.s, j.g))

                step(Job(b, i, 0))
                step(Job(b, i, 1))
                take_first_half(use(b, "QT", i), qt[:, (i + 1) % 2, 0:8, :])
                if i < NT - 1:
                    take_first_half(use(b, "KT", i), kt16[:, (i + 1) % NT, 0:8, :])
                if has_linear(b, i):
                    take_first_half(use(b, "YT", i), yt[:, 0, :, :])

                def body(g):
                    for s in range(2, JPG[i] + 2):
                        step(Job(b, i, s, g))
                    output(b, i, g, jobs0 + JPG[i] * (g + 1))
                    if has_weights(b, i):
                        weights(g)
                group_loop(act, b, i, body)
                if i == NT - 1:
                    take_first_half(use(b, "KT", i), kt16[:, (i + 1) % NT, 0:8, :])
                for q in range(3 * JPG[i] + 2, JOBS[i]):
                    step(Job(b, i, q))
                if i == NT - 1:
                    exponentials(next_job(b, i, 0))
                    exponentials(next_job(b, i, 1))
                prepare()
                if has_weights(b, i):
                    weights(3)
                output(b, i, 3, jobs0 + JOBS[i])

            batches(act, section)
            for k in range(LAG):
                take_first_half(end_turned(k), end_yt[k % 2][:, 0, :, :])
                if k < LAG - 1:
                    y_split(B * NT - LAG + k + 1, end_turned(k))

        @block.vector
        def _(dve):
            def maxima(j):
                dve.wait_ge(slot_filled, j.use.filled)
                if not (isinstance(j.number, int) and j.number < 2):
                    dve.wait_ge(nb_ready, j.number - 1)
                src = slot[:, j.use.slot, :].rearrange("p (h c) -> p h c", c=HEAD_STRIDE[j.i])
                nc.vector.tensor_reduce(mx[:, j.par, 0:j.heads], src[:, 0:j.heads, 0:j.keys], AX_X, ALU.max
                                        ).then_inc(mx_ready, 1)

            def low_parts(j):
                for c in range(j.chunks):
                    dve.wait_ge(hi_ready[c], j.chunk_number(c) + 1)
                    n = (min(4 * c + 4, j.blocks) - 4 * c) * P
                    cols = slice(512 * c, 512 * c + n)
                    nc.vector.tensor_tensor(pt_lo[:, j.par, cols], ptb[:, c, 0:n], pt_hi[:, j.par, cols],
                                            ALU.subtract).then_inc(lo_ready[c], 1)

            def reciprocals(b, i, g, pv):
                gn = 4 * tile(b, i) + g
                if not (isinstance(gn, int) and gn == 0):
                    dve.wait_ge(att_ready, gn)
                dve.wait_ge(pv_done, pv)
                nc.vector.reciprocal(rinv[:, :], rowsum[:, i % 2, bass.ds(GROUP * g, GROUP)]).then_inc(rinv_ready, 1)

            def take_second_half(u, dst):
                dve.wait_ge(slot_filled, u.filled)
                nc.vector.tensor_copy(dst, slot16[:, u.slot, 8:16, :]).then_inc(slot_released[u.slot], 1)

            def moments(k, t, src, s_stats, s_mv, s_rs):
                if not (isinstance(t, int) and t == 0):
                    dve.wait_ge(s_rs, 3 * t)
                for half in range(2):
                    nc.vector.bn_stats(stats[:, k, 6 * half:6 * half + 6], src[:, 512 * half:512 * half + 512]
                                       ).then_inc(s_stats, 1)
                dve_wait_apart(k, s_stats, 2 * t + 2)
                nc.vector.bn_aggr(mv[:, k, :], stats[:, k, :]).then_inc(s_mv, 1)

            def q_moments(t, i, n_in):
                dve.wait_ge(x_in[i % 4], 16 * n_in)
                moments(0, t, ring[:, i % NT, :], q_stats, q_mv, q_rs)

            def q_split(t):
                dve.wait_ge(q_hi, t + 1)
                nc.vector.tensor_tensor(q16[:, :, D:2 * D], norm32[:, :].rearrange("p (h d) -> p h d", d=D),
                                        q16[:, :, 0:D], ALU.subtract).then_inc(q_lo, 1)

            def c_split(t, i):
                dve.wait_ge(c_hi, t + 1)
                nc.vector.tensor_tensor(c16[:, i % 2, :, D:2 * D], cin[:, :].rearrange("p (h d) -> p h d", d=D),
                                        c16[:, i % 2, :, 0:D], ALU.subtract).then_inc(c_lo, 1)

            def y_moments(t, i):
                dve.wait_ge(x1_ready, 4 * t + 4)
                moments(1, t, ring[:, i % NT, :], y_stats, y_mv, y_rs)

            def y_split(t):
                dve.wait_ge(y_hi, t + 1)
                nc.vector.tensor_tensor(y16[:, 1, :, :], norm32[:, :].rearrange("p (k c) -> p k c", c=P),
                                        y16[:, 0, :, :], ALU.subtract).then_inc(y_lo, 1)

            def result(u, t, i):
                dve.wait_ge(slot_filled, u.filled)
                dve.wait_ge(xb_ready, t + 1)
                nc.vector.tensor_tensor(xb[:, i % 2, :], slot[:, u.slot, :], xb[:, i % 2, :], ALU.add
                                        ).then_inc(slot_released[u.slot], 2)

            steps = [0]

            def bias_link(ins):
                steps[0] += 1
                ins.then_inc(bias_step, 1)
                dve.wait_ge(bias_step, steps[0])

            dve.wait_ge(coef_tanh, 1)
            bias_link(nc.vector.tensor_scalar(coef, coef, 0.5, 0.5, ALU.mult, ALU.add))
            bias_link(nc.vector.tensor_tensor(coef, coef, small[:, 0:4], ALU.mult))
            bias_link(nc.vector.tensor_scalar(coef, coef, small[:, 12:13], 0.5, ALU.mult, ALU.mult))
            bias_link(nc.vector.tensor_tensor(bits[:, 0, :], bits[:, 0, :], bits[:, 1, :], ALU.subtract))
            bit = bits[:, 0, :].rearrange("p (j n) -> p j n", n=NBITS)
            bias_link(nc.vector.tensor_scalar(bvec[:, :], bit[:, :, 0], small[:, 4:5], None, ALU.mult))
            for n in range(1, NBITS):
                bias_link(nc.vector.scalar_tensor_tensor(bvec[:, :], bit[:, :, n], small[:, 4 + n:5 + n], bvec[:, :],
                                                         ALU.mult, ALU.add))
            levels = float(2 ** NBITS - 1)
            bias_link(nc.vector.tensor_scalar(bvec[:, :], bvec[:, :], 1.0, -1.0, ALU.min, ALU.max))
            bias_link(nc.vector.tensor_scalar(bvec[:, :], bvec[:, :], levels, ROUND, ALU.mult, ALU.add))
            bias_link(nc.vector.tensor_scalar(bvec[:, :], bvec[:, :], ROUND, 1.0 / levels, ALU.subtract, ALU.mult))
            bias_link(nc.vector.tensor_scalar(bvec[:, :], bvec[:, :], small[:, 13:14], None, ALU.mult))
            assert steps[0] == 12
            dve.wait_ge(pool_const, 10)
            for j in range(8):
                ins = nc.vector.tensor_scalar(bdiag[:, j, :], id32[:, :], bvec[:, j:j + 1], None, ALU.mult)
                if j >= 2:
                    ins.then_inc(bias_step, 1)
            dve.wait_ge(slot_filled, 1)
            nc.vector.tensor_copy(bias_row[:, :].rearrange("p (q j) -> p j q", j=8)[:, 4:8, :],
                                  slot[:, 0, 512:1024].rearrange("p (j q) -> p j q", j=4)
                                  ).then_inc(slot_released[0], 1)
            q_moments(0, 0, 1)
            c_split(0, 0)
            q_split(0)
            take_second_half(Use(1), qt[:, 0, 8:16, :])
            take_second_half(Use(2), kt16[:, 0, 8:16, :])
            q_moments(1, 1, 1)
            c_split(1, 1)
            q_split(1)
            maxima(Job(0, 0, 0))
            maxima(Job(0, 0, 1))

            def section(b, i):
                t = tile(b, i)
                jobs0 = b * JOB0[NT] + JOB0[i]

                def prepare():
                    q_moments(t + 2, i + 2, (i + 2) // 4 + 1 + 2 * b)
                    if has_linear(b, i + 1):
                        y_moments(t - LAG + 1, i - LAG + 1)
                    c_split(t + 2, i + 2)
                    q_split(t + 2)
                    if has_linear(b, i + 1):
                        y_split(t - LAG + 1)

                def weights_sum(n):
                    c = n % NWCH
                    dst = w32[:, c * WCH:(c + 1) * WCH]
                    diff = pairs[n % 4][0].rearrange("p (k n) -> p k n", n=NBITS)
                    dve.wait_ge(d_ready, n + 1)
                    if c == 0 and n > 0:
                        dve.wait_ge(w_lo, n // NWCH)
                    nc.vector.tensor_scalar(dst, diff[:, :, 0], coef[:, 0:1], None, ALU.mult).then_inc(w_step, 1)
                    for k in range(1, NBITS):
                        dve.wait_ge(w_step, NBITS * n + k)
                        nc.vector.scalar_tensor_tensor(dst, diff[:, :, k], coef[:, k:k + 1], dst,
                                                       ALU.mult, ALU.add).then_inc(w_step, 1)

                def weights_low(o):
                    dve.wait_ge(w_hi, o + 1)
                    nc.vector.tensor_tensor(y16[:, 1, :, :], w32.rearrange("p (k c) -> p k c", c=P),
                                            y16[:, 0, :, :], ALU.subtract).then_inc(w_lo, 1)

                def weights(g):
                    k = 4 * i + g
                    if k % 2 and k >= 3:
                        weights_low((k - 3) // 2)
                    for n in (2 * k - 2, 2 * k - 1) if k else ():
                        weights_sum(n)
                    for o in weight_tiles_after(i, g):
                        if o == 7:
                            weights_sum(30)
                            weights_sum(31)
                            weights_low(7)
                        take_second_half(use(b, "WT", o), wt[:, 1, :, o * P:(o + 1) * P])

                def step(j):
                    in_loop = not isinstance(j.g, int)
                    q = None if in_loop else JPG[i] * j.g + j.s
                    if job_ahead(b, i, j.s, j.g):
                        maxima(job_ahead(b, i, j.s, j.g))
                    if in_loop or q < JOBS[i]:
                        low_parts(j)

                def ffn():
                    if has_linear(b, i):
                        result(use(b, "FFN", i), t - LAG, i - LAG)

                step(Job(b, i, 0))
                step(Job(b, i, 1))
                take_second_half(use(b, "QT", i), qt[:, (i + 1) % 2, 8:16, :])
                if i < NT - 1:
                    take_second_half(use(b, "KT", i), kt16[:, (i + 1) % NT, 8:16, :])
                if has_linear(b, i):
                    take_second_half(use(b, "YT", i), yt[:, 1, :, :])

                def body(g):
                    for s in range(2, JPG[i] + 2):
                        step(Job(b, i, s, g))
                    reciprocals(b, i, g, jobs0 + JPG[i] * (g + 1))
                    if has_weights(b, i):
                        weights(g)
                group_loop(dve, b, i, body)
                if i == NT - 1:
                    take_second_half(use(b, "KT", i), kt16[:, (i + 1) % NT, 8:16, :])
                for q in range(3 * JPG[i] + 2, JOBS[i]):
                    step(Job(b, i, q))
                if i == NT - 1:
                    maxima(next_job(b, i, 0))
                    maxima(next_job(b, i, 1))
                prepare()
                if has_weights(b, i):
                    weights(3)
                ffn()
                reciprocals(b, i, 3, jobs0 + JOBS[i])

            batches(dve, section)
            for k in range(LAG):
                t = B * NT - LAG + k
                if k < LAG - 1:
                    y_moments(t + 1, t + 1)
                take_second_half(end_turned(k), end_yt[k % 2][:, 1, :, :])
                if k < LAG - 1:
                    y_split(t + 1)
                if k > 0:
                    result(end_linear(k - 1), t - 1, t - 1)
            result(end_linear(LAG - 1), B * NT - 1, B * NT - 1)

        @block.gpsimd
        def _(pool):
            def deviation(k, t, s_mv, s_rs):
                pool_wait_apart(2 + 3 * k, s_mv, t + 1)
                nc.gpsimd.tensor_scalar(rstd[:, k, 0:1], mv[:, k, 1:2], EPS, None, ALU.add).then_inc(s_rs, 1)
                pool.wait_ge(s_rs, 3 * t + 1)
                nc.gpsimd.tensor_tensor(rstd[:, k, 1:2], rstd[:, k, 0:1], half_neg[:, :], ALU.pow).then_inc(s_rs, 1)
                pool_wait_apart(3 + 3 * k, s_rs, 3 * t + 2)
                nc.gpsimd.tensor_scalar(rstd[:, k, 2:3], mv[:, k, 0:1], rstd[:, k, 1:2], -1.0, ALU.mult, ALU.mult
                                        ).then_inc(s_rs, 1)

            def normalise(k, t, src, last_reader, done):
                if last_reader is not None:
                    pool.wait_ge(*last_reader)
                pool_wait_apart(4 + 3 * k, (q_rs, y_rs)[k], 3 * t + 3)
                nc.gpsimd.tensor_scalar(norm32[:, :], src, rstd[:, k, 1:2], rstd[:, k, 2:3], ALU.mult, ALU.add
                                        ).then_inc(done, 1)

            def add_attention(b, i, g):
                gn = 4 * tile(b, i) + g
                pool.wait_ge(osb_ready, gn + 1)
                if not (isinstance(gn, int) and gn == 0):
                    pool.wait_ge(x1_ready, gn)
                nc.gpsimd.tensor_tensor(att[:, :, :], osb[:, :, 0:D], osb[:, :, D:2 * D], ALU.add).then_inc(osb_added, 1)
                pool.wait_ge(osb_added, gn + 1)
                pool.wait_ge(rinv_ready, gn + 1)
                nc.gpsimd.tensor_tensor(att[:, :, :], att[:, :, :], rinv[:, :].unsqueeze(2).to_broadcast([P, GROUP, D]),
                                        ALU.mult).then_inc(att_ready, 1)
                pool.wait_ge(att_ready, gn + 1)
                dst = ring[:, i % NT, bass.ds(GROUP * D * g, GROUP * D)]
                nc.gpsimd.tensor_tensor(dst, dst, att[:, :, :].rearrange("p h d -> p (h d)"), ALU.add
                                        ).then_inc(x1_ready, 1)

            def add_bias(t, i, n_out):
                if n_out is not None:
                    pool.wait_ge(out_done[i % 2], 16 * n_out)
                nc.gpsimd.tensor_tensor(xb[:, i % 2, :], ring[:, i % NT, :], bias_row[:, :], ALU.add
                                        ).then_inc(xb_ready, 1)

            nc.gpsimd.memset(id32[:, :], 0.0).then_inc(pool_const, 1)
            nc.gpsimd.memset(id16[:, :], 0.0).then_inc(pool_const, 1)
            nc.gpsimd.memset(idb[:, :], 0.0).then_inc(pool_const, 1)
            nc.gpsimd.memset(maskb[:, :], 0.0).then_inc(pool_const, 1)
            nc.gpsimd.memset(ones32[:, :], 1.0).then_inc(pool_const, 1)
            nc.gpsimd.memset(half_neg[:, :], -0.5).then_inc(pool_const, 1)
            pool.wait_ge(pool_const, 6)
            for m in (id32, id16, idb):
                nc.gpsimd.affine_select(out=m[:, :], in_=m[:, :], compare_op=ALU.not_equal, fill=1.0, base=0,
                                        pattern=[[-1, P]], channel_multiplier=1).then_inc(pool_const, 1)
            nc.gpsimd.affine_select(out=maskb[:, :], in_=maskb[:, :], compare_op=ALU.is_ge, fill=MASKED, base=0,
                                    pattern=[[-1, P]], channel_multiplier=1).then_inc(pool_const, 1)
            deviation(0, 0, q_mv, q_rs)
            normalise(0, 0, ring[:, 0, :], (slot_filled, 1), q_norm)
            deviation(0, 1, q_mv, q_rs)
            normalise(0, 1, ring[:, 1, :], (q_lo, 1), q_norm)

            def section(b, i):
                t = tile(b, i)

                def prepare():
                    deviation(0, t + 2, q_mv, q_rs)
                    normalise(0, t + 2, ring[:, (i + 2) % NT, :],
                              (y_lo, t - LAG + 1) if has_linear(b, i) else (q_lo, t + 2), q_norm)
                    if has_linear(b, i + 1):
                        u = t - LAG + 1
                        deviation(1, u, y_mv, y_rs)
                        normalise(1, u, ring[:, (i - LAG + 1) % NT, :], (q_lo, t + 3), y_norm)
                        add_bias(u, i - LAG + 1,
                                 4 * b + (i - LAG + 1) // 2 if has_linear(b, i - 1) else None)

                def weights(g):
                    for n in (8 * i + 2 * g, 8 * i + 2 * g + 1):
                        pool.wait_ge(th_ready, n + 1)
                        nc.gpsimd.tensor_tensor(pairs[n % 4][0], pairs[n % 4][0], pairs[n % 4][1], ALU.subtract
                                                ).then_inc(d_ready, 1)

                def body(g):
                    add_attention(b, i, g)
                    if has_weights(b, i):
                        weights(g)
                group_loop(pool, b, i, body)
                prepare()
                if has_weights(b, i):
                    weights(3)
                add_attention(b, i, 3)

            batches(pool, section)
            for k in range(LAG - 1):
                t = B * NT - LAG + k + 1
                deviation(1, t, y_mv, y_rs)
                normalise(1, t, ring[:, t % NT, :], (y_lo, t), y_norm)
                add_bias(t, t, t // 2)


END_USE = USE_LATER_BASE + (B - 1) * len(USE_LATER)


def end_turned(k):
    return Use(END_USE + max(2 * k - 1, 0))


def end_linear(k):
    return Use(END_USE + min(2 * k + 2, 2 * LAG - 1))


_INS = ['x', 'ctx_2048', 'L0_ffn_pweight', 'L0_ffn_nweight', 'L0_ffn_exps', 'L0_ffn_bexps', 'L0_ffn_mask_weight',
        'L0_ffn_scale', 'L0_ffn_pbias', 'L0_ffn_nbias', 'L0_ffn_biasscale']


def kernel(**inputs):
    import numpy as _np
    import concourse.bacc as _bacc
    from concourse.bass_utils import run_bass_kernel_spmd as _run

    nc = _bacc.Bacc("TRN2", target_bir_lowering=False, num_devices=1)
    arrays, args = {}, []
    for name in _INS:
        a = _np.ascontiguousarray(inputs[name])
        arrays[f"in_{name}_dram"] = a
        args.append(nc.dram_tensor(f"in_{name}_dram", a.shape, mybir.dt.from_np(a.dtype), kind="ExternalInput").ap())
    args.append(nc.dram_tensor("out_0_dram", (B, SEQ, DM), F32, kind="ExternalOutput").ap())
    build(nc, *args)
    r = _run(nc, [arrays], core_ids=[0])
    return r.results[0]["out_0_dram"]
```

```python
import math
from contextlib import ExitStack

import concourse.bass as bass
from concourse import mybir

ALU = mybir.AluOpType
ACT = mybir.ActivationFunctionType
AX_X = mybir.AxisListType.X
F32 = mybir.dt.float32
F16 = mybir.dt.float16
BF16 = mybir.dt.bfloat16

P = 128
B, SEQ, DM = 4, 1024, 1024
NT = SEQ // P
H, D = 16, 64
KT_N = DM // P
NBITS = 4
EPS = 1e-5
SCALE = D ** -0.5
LAG = 5
GROUP = 4
P_SHIFT = 10 * math.log(2)
MASKED = -1e30
ROUND = 1.5 * 2 ** 23

HPJ = [4, 4, 2, 2, 1, 1, 1, 1]
JPG = [GROUP // h for h in HPJ]
JOBS = [H // h for h in HPJ]
JOB0 = [sum(JOBS[:i]) for i in range(NT + 1)]
HEAD_STRIDE = [128, 256, 512, 512, 1024, 1024, 1024, 1024]


CHUNKS = 32


def has_linear(b, i):
    return not (isinstance(b, int) and b == 0 and i < LAG)


def has_weights(b, i):
    return isinstance(b, int) and b == 0 and i < 4


def weight_step(i, g):
    return 4 * i + g + 2


def weight_tiles_after(i, g):
    k = weight_step(i, g)
    return [(k - 3) // 2] if k % 2 else []


def two_parts(i, g):
    return JPG[i] == 2 and g < 3


def looped(i):
    return max(3 * JPG[i], JOBS[i] - 2)


def uses_of(first):
    b = 0 if first else 1
    seq = []

    def scores_ahead(i, steps):
        return [("S", *ahead(i, q)) for q in steps if ahead(i, q)]

    for i in range(NT):
        seq += [("QT", i)] + scores_ahead(i, [1])
        for g in range(3):
            seq += [(name, i) for name in turns(b, i, g)]
            seq += scores_ahead(i, steps_of_group(i, g))
            seq += [("WT", o) for o in weight_tiles_after(i, g)] if has_weights(b, i) else []
        seq += [(name, i) for name in turns(b, i, 3)]
        seq += scores_ahead(i, range(3 * JPG[i] + 2, JOBS[i]))
        seq += [("S", NT, 0), ("S", NT, 1)] if i == NT - 1 else []
        seq += [("WT", o) for o in weight_tiles_after(i, 3)] if has_weights(b, i) else []
        seq += [("FFN", i)] if has_linear(b, i) else []
        seq += [("S", i + 1, 2)]
    return {u: n for n, u in enumerate(seq)}


def turns(b, i, g):
    keys_at = 3 if i == NT - 1 else 2 if JPG[i] == GROUP else 0
    y_at = 2 if i == NT - 1 else {4: 3, 2: 2, 1: 1}[JPG[i]]
    return (["KT"] if g == keys_at else []) + (["YT"] if g == y_at and has_linear(b, i) else [])


def steps_of_group(i, g):
    return range(JPG[i] * g + 2, JPG[i] * g + JPG[i] + 2)


def ahead(i, q):
    if q + 2 < JOBS[i]:
        return i, q + 2
    return (i + 1, q + 2 - JOBS[i]) if q < JOBS[i] and i < NT - 1 else None


USE_FIRST, USE_LATER = uses_of(True), uses_of(False)
USE_BASE = 6
USE_LATER_BASE = USE_BASE + len(USE_FIRST)


class Use:

    def __init__(self, const, run=0):
        self.const, self.run = const, run
        self.slot = const % 2
        self.filled = const - const % 2 + 2 + run
        self.released = const - const % 2 + 2 + run
        self.free = const - const % 2 + run
        self.wait_free = not (isinstance(run, int) and const + run < 2)


def use(b, *key):
    if key[:2] == ("S", 0) and key[2] < 3:
        return Use(USE_BASE - 3 + key[2]) if isinstance(b, int) and b == 0 else use_before(b, "S", NT, key[2])
    if isinstance(b, int) and b == 0:
        return Use(USE_BASE + USE_FIRST[key])
    return Use(USE_LATER_BASE - len(USE_LATER) + USE_LATER[key], len(USE_LATER) * b)


def use_before(b, *key):
    return Use(USE_LATER_BASE - 2 * len(USE_LATER) + USE_LATER[key], len(USE_LATER) * b)


class Job:

    def __init__(self, b, i, s, g=0):
        self.b, self.i, self.s, self.g = b, i, s, g
        static = isinstance(g, int)
        q = JPG[i] * g + s
        self.heads = HPJ[i]
        self.blocks = self.heads * (i + 1)
        self.chunks = (self.blocks + 3) // 4
        self.keys = (i + 1) * P
        self.head0 = GROUP * g + HPJ[i] * s
        self.number = b * JOB0[NT] + JOB0[i] + q
        self.par = (q if static else s) % 2
        self.number1 = b * (JOB0[NT] - JOBS[0]) + JOB0[i] - JOBS[0] + q
        if static:
            self.use = use(b, "S", i, q) if q < JOBS[i] else None
        else:
            base = use(b, "S", i, 4)
            self.use = Use(base.const + s - 4, base.run + JPG[i] * g)

    def chunk_blocks(self, c):
        n = -(-self.blocks // self.chunks)
        return range(n * c, min(n * c + n, self.blocks))

    def chunk_number(self, c):
        return self.number1 if c else self.number


def next_job(b, i, q):
    if i < NT - 1:
        return Job(b, i + 1, q)
    j = Job(b, 0, q)
    j.number = b * JOB0[NT] + JOB0[NT] + q
    j.use = use(b, "S", NT, q)
    return j


def job_ahead(b, i, s, g=0):
    if not isinstance(g, int):
        return Job(b, i, s + 2, g)
    q = JPG[i] * g + s
    if ahead(i, q) is None:
        return None
    return Job(b, i, s + 2, g) if q + 2 < JOBS[i] else next_job(b, i, q + 2 - JOBS[i])


def group_loop(eng, b, i, body, ahead_of):
    ahead_of(0)
    if JPG[i] == 1 or has_weights(b, i):
        for g in range(2):
            if g:
                ahead_of(g)
            body(g)
    else:
        with eng.Fori(0, 2) as g:
            body(g)
    ahead_of(2)
    body(2)
    ahead_of(3)


def batches(eng, section):
    for i in range(NT):
        section(0, i)
    with eng.Fori(1, B) as b:
        for i in range(NT):
            section(b, i)


def build(nc, x, ctx_in, pweight, nweight, exps, bexps, mask_weight, scale, pbias, nbias, biasscale, out):
    x_t = x.rearrange("b (i p) d -> (b i) p d", p=P)
    c_t = ctx_in.rearrange("b (i p) d -> (b i) p d", p=P)
    out_t = out.rearrange("b (i p) d -> (b i) p d", p=P)
    WCH = 256
    NWCH = DM // WCH
    pw_t = pweight.rearrange("(o p) (c k) n -> o c p (k n)", p=P, k=WCH)
    nw_t = nweight.rearrange("(o p) (c k) n -> o c p (k n)", p=P, k=WCH)

    with ExitStack() as stack:
        def sb(name, shape, dt):
            return stack.enter_context(nc.sbuf_tensor(name, shape, dt))

        def sem(name):
            return stack.enter_context(nc.semaphore(name))

        wt = sb("wt", [P, 2, KT_N, DM], F16)
        v16 = sb("v16", [P, NT, H, 2 * D], F16)
        kt16 = sb("kt16", [P, NT, H, P], F16)
        ring = sb("ring", [P, NT, DM], F32)
        cin = sb("cin", [P, DM], F32)
        c16 = sb("c16", [P, 2, H, 2 * D], F16)
        norm32 = sb("norm32", [P, DM], F32)
        q16 = sb("q16", [P, H, 2 * D], F16)
        qt = sb("qt", [P, 2, H, P], F16)
        qs = sb("qs", [P, 2, H, P], F16)
        p32 = sb("p32", [P, 2, 8 * P], F32)
        pt_hi = sb("pt_hi", [P, 2, 8 * P], F16)
        pt_lo = sb("pt_lo", [P, 2, 8 * P], F16)
        osb = sb("osb", [P, GROUP, 2 * D], F32)
        att = sb("att", [P, GROUP, D], F32)
        y16 = sb("y16", [P, 2, KT_N, P], F16)
        yt = sb("yt", [P, 2, KT_N, P], F16)
        xb = sb("xb", [P, 2, DM], F32)
        bias_row = sb("bias_row", [P, DM], F32)
        pairs = [(xb[:, 0, :], xb[:, 1, :])] + [
            tuple(m[:, k].rearrange("p h c -> p (h c)").bitcast(F32) for m, k in two)
            for two in (((v16, 5), (v16, 6)), ((v16, 7), (kt16, 7)), ((kt16, 5), (kt16, 6)))]
        w32 = yt[:, :, :, :].bitcast(F32).rearrange("p a b c -> p (a b c)")
        ones32 = y16[:, 0, 0:2, :].bitcast(F32).rearrange("p a b -> p (a b)")
        end_yt = [yt, v16[:, 4].rearrange("p (a k) c -> p a k c", a=2)]
        id32 = sb("id32", [P, P], F32)
        id16 = sb("id16", [P, P], F16)
        idb = sb("idb", [P, P], BF16)
        maskb = sb("maskb", [P, P], BF16)
        half_neg = sb("half_neg", [P, 1], F32)
        gate = sb("gate", [P, 8], F32)
        mx = sb("mx", [P, 2, GROUP], F32)
        nb = sb("nb", [P, 2, GROUP], F32)
        rowsum = sb("rowsum", [P, 2, H], F32)
        rinv = sb("rinv", [P, GROUP], F32)
        stats = sb("stats", [P, 2, 12], F32)
        mv = sb("mv", [P, 2, 2], F32)
        rstd = sb("rstd", [P, 2, 3], F32)
        small = sb("small", [P, 18], F32)
        coef = small[:, 14:18]
        bits = y16[:, 1, 0, :].bitcast(F32).rearrange("p (a n) -> p a n", a=2)
        bvec = sb("bvec", [P, 8], F32)
        bdiag = norm32[:, :].rearrange("p (j q) -> p j q", j=8)

        slot = stack.enter_context(nc.psum_tensor("slot", [P, 2, 1024], F32))
        ptb = stack.enter_context(nc.psum_tensor("ptb", [P, 2, 512], F32))
        oacc = stack.enter_context(nc.psum_tensor("oacc", [P, 8 * 2 * D], F32))
        slot16 = slot[:, :, :].bitcast(F16).rearrange("p s (k c) -> p s k c", c=P)

        x_in = [sem(f"x_in{r}") for r in range(4)]
        c_in = [sem(f"c_in{r}") for r in range(2)]
        v_in = [sem(f"v_in{r}") for r in range(2)]
        qs_in = [sem(f"qs_in{r}") for r in range(2)]
        w_in = [sem(f"w_in{r}") for r in range(4)]
        out_done = [sem(f"out_done{r}") for r in range(2)]
        small_in = sem("small_in")
        slot_filled = [sem(f"slot_filled{r}") for r in range(2)]
        slot_released = [sem(f"slot_released{r}") for r in range(2)]
        linear_half = sem("linear_half")
        mx_ready = sem("mx_ready")
        nb_ready = sem("nb_ready")
        pt_filled = [sem(f"pt_filled{c}") for c in range(2)]
        hi_ready = [sem(f"hi_ready{c}") for c in range(2)]
        lo_ready = [sem(f"lo_ready{c}") for c in range(2)]
        pv_done = sem("pv_done")
        rinv_ready = sem("rinv_ready")
        osb_ready = sem("osb_ready")
        osb_added = sem("osb_added")
        att_ready = sem("att_ready")
        x1_ready = sem("x1_ready")
        q_stats, q_mv, q_rs, q_norm, q_hi, q_lo = (sem("q_" + n) for n in ("stats", "mv", "rs", "norm", "hi", "lo"))
        c_hi, c_lo = sem("c_hi"), sem("c_lo")
        y_stats, y_mv, y_rs, y_norm, y_hi, y_lo = (sem("y_" + n) for n in ("stats", "mv", "rs", "norm", "hi", "lo"))
        xb_ready = sem("xb_ready")
        pool_const = sem("pool_const")
        th_ready, d_ready, w_step, w_hi, w_lo = (sem("w_" + n) for n in ("tanh", "diff", "step", "hi", "lo"))
        coef_tanh = sem("coef_tanh")
        coef_step = sem("coef_step")
        bias_step = sem("bias_step")

        def tile(b, i):
            return NT * b + i

        def dve_wait_apart(column, s, value):
            nc.vector.wait_ge(s, value)
            nc.vector.memset(gate[:, column:column + 1], 0.0)

        def pool_wait_apart(column, s, value):
            nc.gpsimd.wait_ge(s, value)
            nc.gpsimd.tensor_tensor(gate[:, column:column + 1], half_neg[:, :], half_neg[:, :], ALU.add)

        block = stack.enter_context(nc.Block())

        @block.sync
        def _(sp):
            def load_x(b, k, t):
                if not (isinstance(t, int) and t < NT):
                    sp.wait_ge(xb_ready, t - NT + 1)
                src = x_t[t] if isinstance(t, int) else x_t[bass.ds(t % (B * NT), 1)].rearrange("a p d -> (a p) d")
                sp.dma_start(ring[:, k % NT, :], src).then_inc(x_in[k % 4], 16)

            def load_c(b, k, t):
                if not (isinstance(t, int) and t == 0):
                    sp.wait_ge(c_lo, t)
                src = c_t[t] if isinstance(t, int) else c_t[bass.ds(t % (B * NT), 1)].rearrange("a p d -> (a p) d")
                sp.dma_start(cin[:, :], src).then_inc(c_in[k % 2], 16)

            def keep_v(t, i, pv):
                sp.wait_ge(c_lo, t + 1)
                if pv is not None:
                    sp.wait_ge(pv_done, pv)
                sp.dma_start(v16[:, i % NT], c16[:, i % 2]).then_inc(v_in[i % 2], 16)

            def swap(u, i):
                sp.wait_ge(slot_released[u.slot], u.released)
                sp.dma_start(qs[0:D, i % 2], qt[D:P, i % 2]).then_inc(qs_in[i % 2], 16)
                sp.dma_start(qs[D:P, i % 2], qt[0:D, i % 2]).then_inc(qs_in[i % 2], 16)

            def load_w(n):
                if n >= 4:
                    sp.wait_ge(w_step, NBITS * (n - 3))
                sp.dma_start(pairs[n % 4][0], pw_t[n // NWCH, n % NWCH]).then_inc(w_in[n % 4], 16)
                sp.dma_start(pairs[n % 4][1], nw_t[n // NWCH, n % NWCH]).then_inc(w_in[n % 4], 16)

            for at, src in ((0, exps), (4, bexps), (8, mask_weight), (12, scale), (13, biasscale)):
                n = src.shape[0]
                sp.dma_start(small[:, at:at + n], src.rearrange("(a n) -> a n", a=1).to_broadcast([P, n])
                             ).then_inc(small_in, 16)
            for k, src in enumerate((pbias, nbias)):
                sp.dma_start(bits[:, k, :], src.rearrange("(p j) n -> p (j n)", p=P)).then_inc(small_in, 16)
            load_x(0, 0, 0)
            load_c(0, 0, 0)
            load_x(0, 1, 1)
            for n in range(4):
                load_w(n)
            load_x(0, 2, 2)
            load_c(0, 1, 1)
            swap(Use(1), 0)
            keep_v(0, 0, None)

            def section(b, i):
                t = tile(b, i)
                load_x(b, i + 3, t + 3)
                load_c(b, i + 2, t + 2)
                if isinstance(b, int) and b == 0 and i == 4:
                    sp.wait_ge(w_step, NBITS * CHUNKS)
                if i < NT - 1:
                    keep_v(t + 1, i + 1, None)
                swap(use(b, "QT", i), i + 1)
                if i == NT - 1:
                    keep_v(t + 1, i + 1, b * JOB0[NT] + JOB0[NT])
                if has_weights(b, i):
                    for n in range(8 * i + 6 if i else 4, min(8 * i + 14, CHUNKS)):
                        load_w(n)
                if has_linear(b, i):
                    store(use(b, "FFN", i), t - LAG, i - LAG)

            def store(u, t, k):
                sp.wait_ge(slot_released[u.slot], u.released)
                dst = out_t[t] if isinstance(t, int) else out_t[bass.ds(t, 1)].rearrange("a p d -> (a p) d")
                sp.dma_start(dst, xb[:, k % 2, :]).then_inc(out_done[k % 2], 16)

            batches(sp, section)
            for k in range(LAG):
                t = B * NT - LAG + k
                store(end_linear(k), t, t)
            for r in range(2):
                sp.wait_ge(out_done[r], 16 * B * NT // 2)

        @block.tensor
        def _(pe):
            def take(u):
                if u.wait_free:
                    pe.wait_ge(slot_released[u.slot], u.free)

            def scores(j):
                i = j.i
                take(j.use)
                for hh in range(j.heads):
                    h = j.head0 + hh
                    base = hh * HEAD_STRIDE[i]
                    for w in range((i + 4) // 4):
                        blocks = min(4, i + 1 - 4 * w)
                        dst = slot[:, j.use.slot, base + 512 * w:base + 512 * w + blocks * P]
                        keys = kt16[:, 4 * w:4 * w + blocks, h, :]
                        diagonal = 4 * w + blocks == i + 1
                        pe.matmul(dst, qt[:, i % 2, h, :], keys, start=True, stop=False, skip_group_check=True)
                        last = pe.matmul(dst, qs[:, i % 2, h, :], keys, start=False, stop=not diagonal,
                                         skip_group_check=True)
                        if diagonal:
                            dst = slot[:, j.use.slot, base + i * P:base + (i + 1) * P]
                            last = pe.matmul(dst, idb[:, :], maskb[:, :], start=False, stop=True,
                                             skip_group_check=True)
                last.then_inc(slot_filled[j.use.slot], 2)

            def scores_of_new_tile(b, i, j):
                for name in ("QT", "KT"):
                    u = use(b, name, i)
                    if u.slot != j.use.slot:
                        pe.wait_ge(slot_released[u.slot], u.released)
                n = (i + 1) // 2 + 1 + 4 * b
                pe.wait_ge(qs_in[(i + 1) % 2], 32 * n)
                scores(j)

            def transpose_p(j):
                pe.wait_ge(slot_released[j.use.slot], j.use.released)
                for c in range(j.chunks):
                    n = j.chunk_number(c)
                    if not (isinstance(n, int) and n == 0):
                        pe.wait_ge(lo_ready[c], n)
                    for at, k in enumerate(j.chunk_blocks(c)):
                        last = pe.transpose(ptb[:, c, at * P:(at + 1) * P],
                                            p32[:, j.par, k * P:(k + 1) * P], id32[:, :])
                    last.then_inc(pt_filled[c], 1)

            def values(j, g):
                i = j.i
                first_of_group = (j.s % JPG[i] == 0) if isinstance(j.g, int) else j.s == 0
                gn = 4 * tile(j.b, i) + g
                if first_of_group and not (isinstance(gn, int) and gn < 2):
                    pe.wait_ge(osb_ready, gn - 1)
                for c in range(j.chunks):
                    pe.wait_ge(lo_ready[c], j.chunk_number(c) + 1)
                for hh in range(j.heads):
                    h = j.head0 + hh
                    k0 = (HPJ[i] * j.s + hh) % GROUP
                    at = (g % 2) * (GROUP * 2 * D) + k0 * 2 * D
                    for blk in range(i + 1):
                        k = hh * (i + 1) + blk
                        cols = slice(k * P, (k + 1) * P)
                        pe.matmul(oacc[:, bass.ds(at, 2 * D)], pt_hi[:, j.par, cols], v16[:, blk, h, :],
                                  start=blk == 0, stop=False, skip_group_check=True)
                        last = pe.matmul(oacc[:, bass.ds(at, D)], pt_lo[:, j.par, cols], v16[:, blk, h, 0:D],
                                         start=False, stop=blk == i, skip_group_check=True)
                last.then_inc(pv_done, 1)

            def turn(u, src):
                take(u)
                for k in range(16):
                    last = pe.transpose(slot16[:, u.slot, k, :], src(k), id16[:, :])
                last.then_inc(slot_filled[u.slot], 2)

            def turn_q(u, t):
                pe.wait_ge(q_lo, t + 1)
                turn(u, lambda k: q16[:, k, :])

            def turn_k(u, t, i):
                pe.wait_ge(c_lo, t + 1)
                turn(u, lambda k: c16[:, i % 2, k, :])

            def turn_y(u, t):
                pe.wait_ge(y_lo, t + 1)
                turn(u, lambda k: y16[:, k // KT_N, k % KT_N, :])

            def linear(u, turned, yt, halves=(0, 1)):
                if 0 in halves:
                    take(u)
                    if turned.slot != u.slot:
                        pe.wait_ge(slot_released[turned.slot], turned.released)
                terms = ((0, 0), (1, 0), (0, 1))
                for half in halves:
                    for n, (a, c) in enumerate(terms):
                        for k in range(KT_N):
                            last = pe.matmul(slot[:, u.slot, half * 512:half * 512 + 512], yt[:, a, k, :],
                                             wt[:, c, k, half * 512:half * 512 + 512],
                                             start=n == 0 and k == 0, stop=n == len(terms) - 1 and k == KT_N - 1)
                    if half == 0:
                        last.then_inc(linear_half, 1)
                if 1 in halves:
                    last.then_inc(slot_filled[u.slot], 2)

            pe.wait_ge(pool_const, 10)
            pe.wait_ge(bias_step, 18)
            for j in range(8):
                last = pe.matmul(slot[:, 0, j * P:(j + 1) * P], ones32[:, :], bdiag[:, j, :], start=True, stop=True)
            last.then_inc(slot_filled[0], 2)
            turn_q(Use(1), 0)
            turn_k(Use(2), 0, 0)
            for u in (Use(1), Use(2)):
                pe.wait_ge(slot_released[u.slot], u.released)
            pe.wait_ge(qs_in[0], 32)
            scores(Job(0, 0, 0))
            scores(Job(0, 0, 1))
            transpose_p(Job(0, 0, 0))
            scores(Job(0, 0, 2))

            def section(b, i):
                t = tile(b, i)

                def after_turn(g):
                    return ([2] if g and turns(b, i, g) else []) + (
                        [3 * JPG[i] + 2] if g == 0 and turns(b, i, 3) else [])

                def step(j, g):
                    in_loop = not isinstance(j.g, int)
                    q = None if in_loop else JPG[i] * j.g + j.s
                    coming = job_ahead(b, i, j.s, j.g)
                    new_tile = not in_loop and q + 2 == JOBS[i]
                    late = not in_loop and coming and (j.s in after_turn(j.g) or new_tile and JPG[i] == 1)
                    if coming and new_tile and not late:
                        scores_of_new_tile(b, i, coming)
                    elif coming and not late:
                        scores(coming)
                    if in_loop or q >= 2:
                        values(Job(b, i, j.s - 2, j.g), g)
                    if in_loop or q < JOBS[i]:
                        transpose_p(j)
                    if late and new_tile:
                        scores_of_new_tile(b, i, coming)
                    elif late:
                        scores(coming)

                def ffn(halves):
                    if has_linear(b, i):
                        linear(use(b, "FFN", i), use(b, "YT", i), yt, halves)

                def turn_weights(g):
                    for o in weight_tiles_after(i, g) if has_weights(b, i) else ():
                        pe.wait_ge(w_lo, o + 1)
                        turn(use(b, "WT", o), lambda k: y16[:, k // KT_N, k % KT_N, :])

                def turn_k_y(names):
                    if "KT" in names:
                        turn_k(use(b, "KT", i), t + 1, i + 1)
                    if "YT" in names:
                        turn_y(use(b, "YT", i), t - LAG)

                transpose_p(Job(b, i, 1))
                pe.wait_ge(v_in[i % 2], 16 * (i // 2 + 1 + 4 * b))
                turn_q(use(b, "QT", i), t + 1)
                scores(job_ahead(b, i, 1))

                def body(g):
                    for s in range(2, JPG[i] + 2):
                        step(Job(b, i, s, g), g)
                    if isinstance(g, int):
                        turn_weights(g)
                group_loop(pe, b, i, body, lambda g: turn_k_y(turns(b, i, g)))
                for q in range(3 * JPG[i] + 2, JOBS[i]):
                    step(Job(b, i, q), 3)
                if i == NT - 1:
                    scores_of_new_tile(b, i, next_job(b, i, 0))
                for q in range(looped(i), JOBS[i] - 1):
                    values(Job(b, i, q), 3)
                if i == NT - 1:
                    scores(next_job(b, i, 1))
                turn_weights(3)
                ffn([0])
                values(Job(b, i, JOBS[i] - 1), 3)
                transpose_p(next_job(b, i, 0))
                scores(next_job(b, i, 2))
                ffn([1])

            batches(pe, section)
            turn_y(end_turned(0), B * NT - LAG)
            for k in range(LAG):
                if k < LAG - 1:
                    turn_y(end_turned(k + 1), B * NT - LAG + k + 1)
                linear(end_linear(k), end_turned(k), end_yt[k % 2])

        @block.scalar
        def _(act):
            def exponentials(j):
                act.wait_ge(mx_ready, j.number + 1)
                nc.scalar.activation(nb[:, j.par, 0:j.heads], mx[:, j.par, 0:j.heads], ACT.Copy, bias=P_SHIFT,
                                     scale=-SCALE).then_inc(nb_ready, 1)
                act.wait_ge(nb_ready, j.number + 1)
                for hh in range(j.heads):
                    base = hh * HEAD_STRIDE[j.i]
                    last = nc.scalar.activation(
                        p32[:, j.par, hh * j.keys:(hh + 1) * j.keys], slot[:, j.use.slot, base:base + j.keys],
                        ACT.Exp, bias=nb[:, j.par, hh:hh + 1], scale=SCALE,
                        accum_out=rowsum[:, j.i % 2, bass.ds(j.head0 + hh, 1)])
                last.then_inc(slot_released[j.use.slot], 2)

            def high_parts(j):
                if not (isinstance(j.number, int) and j.number < 2):
                    act.wait_ge(pv_done, j.number - 1)
                for c in range(j.chunks):
                    act.wait_ge(pt_filled[c], j.chunk_number(c) + 1)
                    ks = j.chunk_blocks(c)
                    nc.scalar.copy(pt_hi[:, j.par, P * ks.start:P * ks.stop], ptb[:, c, 0:P * len(ks)]
                                   ).then_inc(hi_ready[c], 1)

            def output(b, i, g, pv):
                gn = 4 * tile(b, i) + g
                if not (isinstance(gn, int) and gn == 0):
                    act.wait_ge(osb_added, gn)
                act.wait_ge(pv_done, pv)
                nc.scalar.copy(osb[:, :, :].rearrange("p k c -> p (k c)"),
                               oacc[:, bass.ds((g % 2) * GROUP * 2 * D, GROUP * 2 * D)]).then_inc(osb_ready, 1)

            def take_first_half(u, dst):
                act.wait_ge(slot_filled[u.slot], u.filled)
                nc.scalar.copy(dst, slot16[:, u.slot, 0:8, :]).then_inc(slot_released[u.slot], 1)

            def q_split(t, i, turned):
                act.wait_ge(q_norm, t + 1)
                if turned is not None:
                    act.wait_ge(slot_filled[turned.slot], turned.filled)
                nc.scalar.copy(q16[:, :, 0:D], norm32[:, :].rearrange("p (h d) -> p h d", d=D)).then_inc(q_hi, 1)

            def c_split(t, i, turned, n_in):
                act.wait_ge(c_in[i % 2], 16 * n_in)
                if turned is not None:
                    act.wait_ge(slot_filled[turned.slot], turned.filled)
                    act.wait_ge(v_in[i % 2], 16 * (n_in - 1))
                nc.scalar.copy(c16[:, i % 2, :, 0:D], cin[:, :].rearrange("p (h d) -> p h d", d=D)
                               ).then_inc(c_hi, 1)

            def y_split(t, turned):
                act.wait_ge(y_norm, t + 1)
                if turned is not None:
                    act.wait_ge(slot_filled[turned.slot], turned.filled)
                nc.scalar.copy(y16[:, 0, :, :], norm32[:, :].rearrange("p (k c) -> p k c", c=P)).then_inc(y_hi, 1)

            def chunk_tanh(n):
                if n >= CHUNKS:
                    return
                act.wait_ge(w_in[n % 4], 32 * (n // 4 + 1))
                for half in pairs[n % 4]:
                    last = nc.scalar.activation(half, half, ACT.Tanh, scale=0.5)
                last.then_inc(th_ready, 1)

            act.wait_ge(small_in, 16 * 7)
            nc.scalar.activation(coef, small[:, 8:12], ACT.Tanh, scale=0.5).then_inc(coef_tanh, 1)
            c_split(0, 0, None, 1)
            chunk_tanh(0)
            chunk_tanh(1)
            q_split(0, 0, None)
            act.wait_ge(slot_filled[0], Use(0).filled)
            nc.scalar.copy(bias_row[:, :].rearrange("p (q j) -> p j q", j=8)[:, 0:4, :],
                           slot[:, 0, 0:512].rearrange("p (j q) -> p j q", j=4)).then_inc(slot_released[0], 1)
            take_first_half(Use(1), qt[:, 0, 0:8, :])
            take_first_half(Use(2), kt16[:, 0, 0:8, :])
            c_split(1, 1, None, 1)
            chunk_tanh(2)
            q_split(1, 1, Use(1))
            chunk_tanh(3)
            exponentials(Job(0, 0, 0))
            exponentials(Job(0, 0, 1))
            high_parts(Job(0, 0, 0))
            exponentials(Job(0, 0, 2))

            def section(b, i):
                first = isinstance(b, int) and b == 0
                t = tile(b, i)
                jobs0 = b * JOB0[NT] + JOB0[i]

                def prepare():
                    if i > 0:
                        c_turned = use(b, "KT", i - 1)
                    else:
                        c_turned = Use(2) if first else use_before(b, "KT", NT - 1)
                    q_split(t + 2, i + 2, use(b, "QT", i))
                    c_split(t + 2, i + 2, c_turned, (i + 2) // 2 + 1 + 4 * b)
                    if has_linear(b, i + 1):
                        y_split(t - LAG + 1, None if not has_linear(b, i) else use(b, "YT", i))

                def weights_high(o):
                    act.wait_ge(w_step, NBITS * NWCH * (o + 1))
                    if o > 0:
                        turned = use(0, "WT", o - 1)
                        act.wait_ge(slot_filled[turned.slot], turned.filled)
                    nc.scalar.copy(y16[:, 0, :, :], w32.rearrange("p (k c) -> p k c", c=P)).then_inc(w_hi, 1)

                def weights(g):
                    k = weight_step(i, g)
                    if not two_parts(i, g):
                        chunk_tanh(2 * k)
                    chunk_tanh(2 * k + 1)
                    if k % 2 == 0:
                        weights_high((k - 2) // 2)
                    for o in weight_tiles_after(i, g):
                        take_first_half(use(b, "WT", o), wt[:, 0, :, o * P:(o + 1) * P])

                def step(j):
                    in_loop = not isinstance(j.g, int)
                    q = None if in_loop else JPG[i] * j.g + j.s
                    if in_loop or q < JOBS[i]:
                        high_parts(j)
                    if job_ahead(b, i, j.s, j.g):
                        exponentials(job_ahead(b, i, j.s, j.g))

                def take_k_y(names):
                    if "KT" in names:
                        take_first_half(use(b, "KT", i), kt16[:, (i + 1) % NT, 0:8, :])
                    if "YT" in names:
                        take_first_half(use(b, "YT", i), yt[:, 0, :, :])

                high_parts(Job(b, i, 1))
                take_first_half(use(b, "QT", i), qt[:, (i + 1) % 2, 0:8, :])
                exponentials(job_ahead(b, i, 1))

                def body(g):
                    for s in range(2, JPG[i] + 2):
                        step(Job(b, i, s, g))
                        if s == 2 and has_weights(b, i) and two_parts(i, g):
                            chunk_tanh(2 * weight_step(i, g))
                    output(b, i, g, jobs0 + JPG[i] * (g + 1))
                    if has_weights(b, i):
                        weights(g)
                group_loop(act, b, i, body, lambda g: take_k_y(turns(b, i, g)))
                for q in range(3 * JPG[i] + 2, JOBS[i]):
                    step(Job(b, i, q))
                if i == NT - 1:
                    exponentials(next_job(b, i, 0))
                    exponentials(next_job(b, i, 1))
                prepare()
                if has_weights(b, i):
                    weights(3)
                output(b, i, 3, jobs0 + JOBS[i])
                high_parts(next_job(b, i, 0))
                exponentials(next_job(b, i, 2))

            batches(act, section)
            for k in range(LAG):
                take_first_half(end_turned(k), end_yt[k % 2][:, 0, :, :])
                if k < LAG - 1:
                    y_split(B * NT - LAG + k + 1, end_turned(k))

        @block.vector
        def _(dve):
            def maxima(j):
                dve.wait_ge(slot_filled[j.use.slot], j.use.filled)
                if not (isinstance(j.number, int) and j.number < 2):
                    dve.wait_ge(nb_ready, j.number - 1)
                src = slot[:, j.use.slot, :].rearrange("p (h c) -> p h c", c=HEAD_STRIDE[j.i])
                nc.vector.tensor_reduce(mx[:, j.par, 0:j.heads], src[:, 0:j.heads, 0:j.keys], AX_X, ALU.max
                                        ).then_inc(mx_ready, 1)

            def low_parts(j):
                for c in range(j.chunks):
                    dve.wait_ge(hi_ready[c], j.chunk_number(c) + 1)
                    ks = j.chunk_blocks(c)
                    cols = slice(P * ks.start, P * ks.stop)
                    nc.vector.tensor_tensor(pt_lo[:, j.par, cols], ptb[:, c, 0:P * len(ks)], pt_hi[:, j.par, cols],
                                            ALU.subtract).then_inc(lo_ready[c], 1)

            def reciprocals(b, i, g, pv):
                gn = 4 * tile(b, i) + g
                if not (isinstance(gn, int) and gn == 0):
                    dve.wait_ge(att_ready, gn)
                dve.wait_ge(pv_done, pv)
                nc.vector.reciprocal(rinv[:, :], rowsum[:, i % 2, bass.ds(GROUP * g, GROUP)]).then_inc(rinv_ready, 1)

            def take_second_half(u, dst):
                dve.wait_ge(slot_filled[u.slot], u.filled)
                nc.vector.tensor_copy(dst, slot16[:, u.slot, 8:16, :]).then_inc(slot_released[u.slot], 1)

            def moments(k, t, src, s_stats, s_mv, s_rs):
                if not (isinstance(t, int) and t == 0):
                    dve.wait_ge(s_rs, 3 * t)
                for half in range(2):
                    nc.vector.bn_stats(stats[:, k, 6 * half:6 * half + 6], src[:, 512 * half:512 * half + 512]
                                       ).then_inc(s_stats, 1)
                dve_wait_apart(k, s_stats, 2 * t + 2)
                nc.vector.bn_aggr(mv[:, k, :], stats[:, k, :]).then_inc(s_mv, 1)

            def q_moments(t, i, n_in):
                dve.wait_ge(x_in[i % 4], 16 * n_in)
                moments(0, t, ring[:, i % NT, :], q_stats, q_mv, q_rs)

            def q_split(t):
                dve.wait_ge(q_hi, t + 1)
                nc.vector.tensor_tensor(q16[:, :, D:2 * D], norm32[:, :].rearrange("p (h d) -> p h d", d=D),
                                        q16[:, :, 0:D], ALU.subtract).then_inc(q_lo, 1)

            def c_split(t, i):
                dve.wait_ge(c_hi, t + 1)
                nc.vector.tensor_tensor(c16[:, i % 2, :, D:2 * D], cin[:, :].rearrange("p (h d) -> p h d", d=D),
                                        c16[:, i % 2, :, 0:D], ALU.subtract).then_inc(c_lo, 1)

            def y_moments(t, i):
                dve.wait_ge(x1_ready, 4 * t + 4)
                moments(1, t, ring[:, i % NT, :], y_stats, y_mv, y_rs)

            def y_split(t):
                dve.wait_ge(y_hi, t + 1)
                nc.vector.tensor_tensor(y16[:, 1, :, :], norm32[:, :].rearrange("p (k c) -> p k c", c=P),
                                        y16[:, 0, :, :], ALU.subtract).then_inc(y_lo, 1)

            def result(u, t, i, half):
                if half == 0:
                    dve.wait_ge(linear_half, t + 1)
                    dve.wait_ge(xb_ready, t + 1)
                else:
                    dve.wait_ge(slot_filled[u.slot], u.filled)
                cols = slice(512 * half, 512 * half + 512)
                ins = nc.vector.tensor_tensor(xb[:, i % 2, cols], slot[:, u.slot, cols], xb[:, i % 2, cols], ALU.add)
                if half == 1:
                    ins.then_inc(slot_released[u.slot], 2)

            def weights_sum(n):
                if n >= CHUNKS:
                    return
                c = n % NWCH
                dst = w32[:, c * WCH:(c + 1) * WCH]
                diff = pairs[n % 4][0].rearrange("p (k n) -> p k n", n=NBITS)
                dve.wait_ge(d_ready, n + 1)
                if c == 0 and n > 0:
                    dve.wait_ge(w_lo, n // NWCH)
                nc.vector.tensor_scalar(dst, diff[:, :, 0], coef[:, 0:1], None, ALU.mult).then_inc(w_step, 1)
                for k in range(1, NBITS):
                    dve.wait_ge(w_step, NBITS * n + k)
                    nc.vector.scalar_tensor_tensor(dst, diff[:, :, k], coef[:, k:k + 1], dst,
                                                   ALU.mult, ALU.add).then_inc(w_step, 1)

            steps = [0]

            def bias_link(ins):
                steps[0] += 1
                ins.then_inc(bias_step, 1)
                dve.wait_ge(bias_step, steps[0])

            dve.wait_ge(coef_tanh, 1)
            bias_link(nc.vector.tensor_scalar(coef, coef, 0.5, 0.5, ALU.mult, ALU.add))
            bias_link(nc.vector.tensor_tensor(coef, coef, small[:, 0:4], ALU.mult))
            bias_link(nc.vector.tensor_scalar(coef, coef, small[:, 12:13], 0.5, ALU.mult, ALU.mult))
            bias_link(nc.vector.tensor_tensor(bits[:, 0, :], bits[:, 0, :], bits[:, 1, :], ALU.subtract))
            bit = bits[:, 0, :].rearrange("p (j n) -> p j n", n=NBITS)
            bias_link(nc.vector.tensor_scalar(bvec[:, :], bit[:, :, 0], small[:, 4:5], None, ALU.mult))
            for n in range(1, NBITS):
                bias_link(nc.vector.scalar_tensor_tensor(bvec[:, :], bit[:, :, n], small[:, 4 + n:5 + n], bvec[:, :],
                                                         ALU.mult, ALU.add))
            levels = float(2 ** NBITS - 1)
            bias_link(nc.vector.tensor_scalar(bvec[:, :], bvec[:, :], 1.0, -1.0, ALU.min, ALU.max))
            bias_link(nc.vector.tensor_scalar(bvec[:, :], bvec[:, :], levels, ROUND, ALU.mult, ALU.add))
            bias_link(nc.vector.tensor_scalar(bvec[:, :], bvec[:, :], ROUND, 1.0 / levels, ALU.subtract, ALU.mult))
            bias_link(nc.vector.tensor_scalar(bvec[:, :], bvec[:, :], small[:, 13:14], None, ALU.mult))
            assert steps[0] == 12
            dve.wait_ge(pool_const, 10)
            for j in range(8):
                ins = nc.vector.tensor_scalar(bdiag[:, j, :], id32[:, :], bvec[:, j:j + 1], None, ALU.mult)
                if j >= 2:
                    ins.then_inc(bias_step, 1)
            dve.wait_ge(slot_filled[0], Use(0).filled)
            nc.vector.tensor_copy(bias_row[:, :].rearrange("p (q j) -> p j q", j=8)[:, 4:8, :],
                                  slot[:, 0, 512:1024].rearrange("p (j q) -> p j q", j=4)
                                  ).then_inc(slot_released[0], 1)
            q_moments(0, 0, 1)
            c_split(0, 0)
            weights_sum(0)
            q_split(0)
            take_second_half(Use(1), qt[:, 0, 8:16, :])
            take_second_half(Use(2), kt16[:, 0, 8:16, :])
            q_moments(1, 1, 1)
            c_split(1, 1)
            weights_sum(1)
            q_split(1)
            maxima(Job(0, 0, 0))
            q_moments(2, 2, 1)
            maxima(Job(0, 0, 1))
            maxima(Job(0, 0, 2))
            low_parts(Job(0, 0, 0))

            def section(b, i):
                t = tile(b, i)
                jobs0 = b * JOB0[NT] + JOB0[i]

                def prepare():
                    q_split(t + 2)
                    c_split(t + 2, i + 2)
                    q_moments(t + 3, i + 3, (i + 3) // 4 + 1 + 2 * b)
                    if has_linear(b, i + 1):
                        y_split(t - LAG + 1)

                def weights_low(o):
                    dve.wait_ge(w_hi, o + 1)
                    nc.vector.tensor_tensor(y16[:, 1, :, :], w32.rearrange("p (k c) -> p k c", c=P),
                                            y16[:, 0, :, :], ALU.subtract).then_inc(w_lo, 1)

                def weights_low_and_sum(k):
                    if k % 2:
                        weights_low((k - 3) // 2)
                    weights_sum(2 * k - 2)

                def weights(g):
                    k = weight_step(i, g)
                    if not two_parts(i, g):
                        weights_low_and_sum(k)
                    weights_sum(2 * k - 1)
                    for o in weight_tiles_after(i, g):
                        take_second_half(use(b, "WT", o), wt[:, 1, :, o * P:(o + 1) * P])

                def step(j):
                    in_loop = not isinstance(j.g, int)
                    q = None if in_loop else JPG[i] * j.g + j.s
                    late = JPG[i] == 1 and q + 2 == JOBS[i]
                    if late:
                        low_parts(j)
                    if job_ahead(b, i, j.s, j.g):
                        maxima(job_ahead(b, i, j.s, j.g))
                    if in_loop or q < JOBS[i] and not late:
                        low_parts(j)

                def ffn(half):
                    if has_linear(b, i):
                        result(use(b, "FFN", i), t - LAG, i - LAG, half)

                def take_k_y(names):
                    if "KT" in names:
                        take_second_half(use(b, "KT", i), kt16[:, (i + 1) % NT, 8:16, :])
                    if "YT" in names:
                        take_second_half(use(b, "YT", i), yt[:, 1, :, :])

                low_parts(Job(b, i, 1))
                take_second_half(use(b, "QT", i), qt[:, (i + 1) % 2, 8:16, :])
                maxima(job_ahead(b, i, 1))

                def body(g):
                    for s in range(2, JPG[i] + 2):
                        step(Job(b, i, s, g))
                        if s == 2 and has_weights(b, i) and two_parts(i, g):
                            weights_low_and_sum(weight_step(i, g))
                    reciprocals(b, i, g, jobs0 + JPG[i] * (g + 1))
                    if has_weights(b, i):
                        weights(g)
                group_loop(dve, b, i, body, lambda g: take_k_y(turns(b, i, g)))
                for q in range(3 * JPG[i] + 2, JOBS[i]):
                    step(Job(b, i, q))
                if i == NT - 1:
                    maxima(next_job(b, i, 0))
                    maxima(next_job(b, i, 1))
                prepare()
                if has_weights(b, i):
                    weights(3)
                reciprocals(b, i, 3, jobs0 + JOBS[i])
                low_parts(next_job(b, i, 0))
                maxima(next_job(b, i, 2))
                ffn(0)
                if has_linear(b, i + 2):
                    y_moments(t - LAG + 2, i - LAG + 2)
                ffn(1)

            batches(dve, section)
            for k in range(LAG):
                t = B * NT - LAG + k
                if 0 < k < LAG - 1:
                    y_moments(t + 1, t + 1)
                take_second_half(end_turned(k), end_yt[k % 2][:, 1, :, :])
                if k < LAG - 1:
                    y_split(t + 1)
                if k > 0:
                    for half in range(2):
                        result(end_linear(k - 1), t - 1, t - 1, half)
            for half in range(2):
                result(end_linear(LAG - 1), B * NT - 1, B * NT - 1, half)

        @block.gpsimd
        def _(pool):
            def deviation(k, t, s_mv, s_rs):
                pool_wait_apart(2 + 3 * k, s_mv, t + 1)
                nc.gpsimd.tensor_scalar(rstd[:, k, 0:1], mv[:, k, 1:2], EPS, None, ALU.add).then_inc(s_rs, 1)
                pool.wait_ge(s_rs, 3 * t + 1)
                nc.gpsimd.tensor_tensor(rstd[:, k, 1:2], rstd[:, k, 0:1], half_neg[:, :], ALU.pow).then_inc(s_rs, 1)
                pool_wait_apart(3 + 3 * k, s_rs, 3 * t + 2)
                nc.gpsimd.tensor_scalar(rstd[:, k, 2:3], mv[:, k, 0:1], rstd[:, k, 1:2], -1.0, ALU.mult, ALU.mult
                                        ).then_inc(s_rs, 1)

            def normalise(k, t, src, last_reader, done):
                if last_reader is not None:
                    pool.wait_ge(*last_reader)
                pool_wait_apart(4 + 3 * k, (q_rs, y_rs)[k], 3 * t + 3)
                nc.gpsimd.tensor_scalar(norm32[:, :], src, rstd[:, k, 1:2], rstd[:, k, 2:3], ALU.mult, ALU.add
                                        ).then_inc(done, 1)

            def add_attention(b, i, g):
                gn = 4 * tile(b, i) + g
                pool.wait_ge(osb_ready, gn + 1)
                if not (isinstance(gn, int) and gn == 0):
                    pool.wait_ge(x1_ready, gn)
                nc.gpsimd.tensor_tensor(att[:, :, :], osb[:, :, 0:D], osb[:, :, D:2 * D], ALU.add).then_inc(osb_added, 1)
                pool.wait_ge(osb_added, gn + 1)
                pool.wait_ge(rinv_ready, gn + 1)
                nc.gpsimd.tensor_tensor(att[:, :, :], att[:, :, :], rinv[:, :].unsqueeze(2).to_broadcast([P, GROUP, D]),
                                        ALU.mult).then_inc(att_ready, 1)
                pool.wait_ge(att_ready, gn + 1)
                dst = ring[:, i % NT, bass.ds(GROUP * D * g, GROUP * D)]
                nc.gpsimd.tensor_tensor(dst, dst, att[:, :, :].rearrange("p h d -> p (h d)"), ALU.add
                                        ).then_inc(x1_ready, 1)

            def add_bias(t, i, n_out):
                if n_out is not None:
                    pool.wait_ge(out_done[i % 2], 16 * n_out)
                nc.gpsimd.tensor_tensor(xb[:, i % 2, :], ring[:, i % NT, :], bias_row[:, :], ALU.add
                                        ).then_inc(xb_ready, 1)

            def difference(n):
                if n >= CHUNKS:
                    return
                pool.wait_ge(th_ready, n + 1)
                nc.gpsimd.tensor_tensor(pairs[n % 4][0], pairs[n % 4][0], pairs[n % 4][1], ALU.subtract
                                        ).then_inc(d_ready, 1)

            nc.gpsimd.memset(id32[:, :], 0.0).then_inc(pool_const, 1)
            nc.gpsimd.memset(id16[:, :], 0.0).then_inc(pool_const, 1)
            nc.gpsimd.memset(idb[:, :], 0.0).then_inc(pool_const, 1)
            nc.gpsimd.memset(maskb[:, :], 0.0).then_inc(pool_const, 1)
            nc.gpsimd.memset(ones32[:, :], 1.0).then_inc(pool_const, 1)
            nc.gpsimd.memset(half_neg[:, :], -0.5).then_inc(pool_const, 1)
            pool.wait_ge(pool_const, 6)
            for m in (id32, id16, idb):
                nc.gpsimd.affine_select(out=m[:, :], in_=m[:, :], compare_op=ALU.not_equal, fill=1.0, base=0,
                                        pattern=[[-1, P]], channel_multiplier=1).then_inc(pool_const, 1)
            nc.gpsimd.affine_select(out=maskb[:, :], in_=maskb[:, :], compare_op=ALU.is_ge, fill=MASKED, base=0,
                                    pattern=[[-1, P]], channel_multiplier=1).then_inc(pool_const, 1)
            difference(0)
            deviation(0, 0, q_mv, q_rs)
            normalise(0, 0, ring[:, 0, :], (slot_filled[0], Use(0).filled), q_norm)
            difference(1)
            deviation(0, 1, q_mv, q_rs)
            normalise(0, 1, ring[:, 1, :], (q_lo, 1), q_norm)
            difference(2)
            difference(3)

            def section(b, i):
                t = tile(b, i)

                def prepare_moments():
                    deviation(0, t + 2, q_mv, q_rs)
                    if has_linear(b, i + 1):
                        deviation(1, t - LAG + 1, y_mv, y_rs)
                    normalise(0, t + 2, ring[:, (i + 2) % NT, :],
                              (y_lo, t - LAG + 1) if has_linear(b, i) else (q_lo, t + 2), q_norm)

                def prepare():
                    if has_linear(b, i + 1):
                        u = t - LAG + 1
                        normalise(1, u, ring[:, (i - LAG + 1) % NT, :], (q_lo, t + 3), y_norm)
                        add_bias(u, i - LAG + 1,
                                 4 * b + (i - LAG + 1) // 2 if has_linear(b, i - 1) else None)

                def body(g):
                    if has_weights(b, i) and two_parts(i, g):
                        difference(2 * weight_step(i, g))
                    add_attention(b, i, g)
                    if has_weights(b, i):
                        weights(g)

                def weights(g):
                    k = weight_step(i, g)
                    if not two_parts(i, g):
                        difference(2 * k)
                    difference(2 * k + 1)

                group_loop(pool, b, i, body, lambda g: prepare_moments() if g == 0 else None)
                prepare()
                if has_weights(b, i):
                    weights(3)
                add_attention(b, i, 3)

            batches(pool, section)
            for k in range(LAG - 1):
                t = B * NT - LAG + k + 1
                deviation(1, t, y_mv, y_rs)
                normalise(1, t, ring[:, t % NT, :], (y_lo, t), y_norm)
                add_bias(t, t, t // 2)


END_USE = USE_LATER_BASE + (B - 1) * len(USE_LATER)


def end_turned(k):
    return Use(END_USE + max(2 * k - 1, 0))


def end_linear(k):
    return Use(END_USE + min(2 * k + 2, 2 * LAG - 1))


_INS = ['x', 'ctx_2048', 'L0_ffn_pweight', 'L0_ffn_nweight', 'L0_ffn_exps', 'L0_ffn_bexps', 'L0_ffn_mask_weight',
        'L0_ffn_scale', 'L0_ffn_pbias', 'L0_ffn_nbias', 'L0_ffn_biasscale']


def kernel(**inputs):
    import numpy as _np
    import concourse.bacc as _bacc
    from concourse.bass_utils import run_bass_kernel_spmd as _run

    nc = _bacc.Bacc("TRN2", target_bir_lowering=False, num_devices=1)
    arrays, args = {}, []
    for name in _INS:
        a = _np.ascontiguousarray(inputs[name])
        arrays[f"in_{name}_dram"] = a
        args.append(nc.dram_tensor(f"in_{name}_dram", a.shape, mybir.dt.from_np(a.dtype), kind="ExternalInput").ap())
    args.append(nc.dram_tensor("out_0_dram", (B, SEQ, DM), F32, kind="ExternalOutput").ap())
    build(nc, *args)
    r = _run(nc, [arrays], core_ids=[0])
    return r.results[0]["out_0_dram"]
```
